# Optimizing a Trainium2 kernel written in Bass

```python
import numpy as np
import jax
import jax.numpy as jnp

def _softmax(x, axis=-1):
    return jax.nn.softmax(x, axis=axis)

def _gelu(x):
    return jax.nn.gelu(x, approximate=True)

def _silu(x):
    return jax.nn.silu(x)

def _sigmoid(x):
    return jax.nn.sigmoid(x)

def _layernorm(x, axis=-1, eps=1e-05):
    m = jnp.mean(x, axis=axis, keepdims=True)
    v = jnp.var(x, axis=axis, keepdims=True)
    return (x - m) / jnp.sqrt(v + eps)

def _scatter_add(tgt, idx, src, axis=0):
    return tgt.at[idx].add(src)

def _segment_sum(src, seg, n):
    return jax.ops.segment_sum(src, seg, n)
kernel_name = 'mk_sandwich_d1_jaxref_r4_087db0'

def setup_inputs(seed: int=0):
    np.random.seed(seed)
    _w = jnp.asarray

    def _L0_attn_setup():
        import jax, jax.numpy as jnp
        import numpy as np
        N_EMBED = 512
        N_HEAD = 16
        HEAD_DIM = N_EMBED // N_HEAD

        def _rotate(x):
            x1, x2 = jnp.split(x, 2, axis=-1)
            return jnp.concatenate((-x2, x1), axis=-1)
        key = jax.random.key(seed)
        k1, k2, k3 = jax.random.split(key, 3)
        B, T = (2, 512)
        x = jax.random.normal(k1, (B, T, N_EMBED), dtype=jnp.float32)
        w_attn = jax.random.normal(k2, ((N_HEAD + 2) * HEAD_DIM, N_EMBED), dtype=jnp.float32) * 0.02
        w_out = jax.random.normal(k3, (N_EMBED, N_EMBED), dtype=jnp.float32) * 0.02
        return {'x': x, 'w_attn': w_attn, 'w_out': w_out}
    _L0_attn_in = _L0_attn_setup()

    def _L0_ffn_setup():
        import jax, jax.numpy as jnp
        import numpy as np
        key = jax.random.key(seed)
        k1, k2, k3, k4 = jax.random.split(key, 4)
        B, S, D_IN, D_OUT = (4, 1024, 512, 512)
        x = jax.random.normal(k1, (B, S, D_IN), dtype=jnp.float32)
        weight = jax.random.normal(k2, (D_OUT, D_IN), dtype=jnp.float32) * 0.02
        scale_weight = jax.random.uniform(k3, (D_OUT,), dtype=jnp.float32, minval=0.5, maxval=1.5)
        bias = jax.random.normal(k4, (D_OUT,), dtype=jnp.float32) * 0.02
        return {'x': x, 'weight': weight, 'scale_weight': scale_weight, 'bias': bias}
    _L0_ffn_in = _L0_ffn_setup()
    _d = {'L0_attn_x': _L0_attn_in['x'], 'L0_attn_w_attn': _L0_attn_in['w_attn'], 'L0_attn_w_out': _L0_attn_in['w_out'], 'L0_ffn_weight': _L0_ffn_in['weight'], 'L0_ffn_scale_weight': _L0_ffn_in['scale_weight'], 'L0_ffn_bias': _L0_ffn_in['bias']}
    _x0 = _d['L0_attn_x']
    _d['L0_attn_x'] = jax.random.normal(jax.random.fold_in(jax.random.key(seed), 1), (1, 2048, 512), dtype=_x0.dtype)
    del _x0
    return _d

def reference(L0_attn_x, L0_attn_w_attn, L0_attn_w_out, L0_ffn_weight, L0_ffn_scale_weight, L0_ffn_bias):

    def _L0_attn_ref(x, w_attn, w_out):
        import jax, jax.numpy as jnp
        import numpy as np
        N_EMBED = 512
        N_HEAD = 16
        HEAD_DIM = N_EMBED // N_HEAD

        def _rotate(x):
            x1, x2 = jnp.split(x, 2, axis=-1)
            return jnp.concatenate((-x2, x1), axis=-1)
        B, T, _ = x.shape
        qkv = x @ w_attn.T
        q, k, v = jnp.split(qkv, [N_EMBED, N_EMBED + HEAD_DIM], axis=2)
        q = q.reshape(B, T, N_HEAD, HEAD_DIM).transpose(0, 2, 1, 3)
        k = k.reshape(B, T, HEAD_DIM)
        v = v.reshape(B, T, HEAD_DIM)
        pos = jnp.asarray(10000.0 ** ((-2.0 * np.arange(0, HEAD_DIM, 2) - 1.0) / HEAD_DIM), dtype=x.dtype)
        angles = jnp.arange(T, dtype=x.dtype)[:, None] * pos[None, :]
        rot = jnp.concatenate((angles, angles), axis=-1)
        cos, sin = (jnp.cos(rot), jnp.sin(rot))
        q = q * cos + _rotate(q) * sin
        k = k * cos + _rotate(k) * sin
        scores = jnp.einsum('bhqd,bkd->bhqk', q, k) * HEAD_DIM ** (-0.5)
        attn = jax.nn.softmax(scores, axis=-1)
        out = jnp.einsum('bhqk,bkd->bhqd', attn, v)
        out = out.transpose(0, 2, 1, 3).reshape(B, T, N_EMBED)
        return out @ w_out.T

    def _L0_ffn_ref(x, weight, scale_weight, bias):
        import jax, jax.numpy as jnp
        import numpy as np
        w = weight * scale_weight[:, None]
        out = jnp.einsum('bsi,oi->bso', x, w) + bias
        return out
    x = L0_attn_x
    x = x + _layernorm(_L0_attn_ref(_layernorm(x, axis=-1), L0_attn_w_attn, L0_attn_w_out), axis=-1)
    x = x + _layernorm(_L0_ffn_ref(_layernorm(x, axis=-1), L0_ffn_weight, L0_ffn_scale_weight, L0_ffn_bias), axis=-1)
    return x

_drawn_inputs = setup_inputs


def setup_inputs(seed=0):
    import zlib

    import numpy as np

    out = dict(_drawn_inputs(seed))
    spreads = {}
    factors = {}
    for name, (base, spread) in spreads.items():
        noise = np.random.default_rng([zlib.crc32(name.encode()), seed]).standard_normal(out[name].shape)
        drawn = base * np.exp(spread * noise) if base else spread * noise
        out[name] = jnp.asarray(drawn.astype(out[name].dtype))
    for name, factor in factors.items():
        out[name] = (out[name] * factor).astype(out[name].dtype)
    return out
```

```python
from contextlib import ExitStack

import concourse.bass as bass
from concourse import mybir

F32 = mybir.dt.float32
F32R = mybir.dt.float32r
ALU = mybir.AluOpType
ACT = mybir.ActivationFunctionType
AX = mybir.AxisListType

P = 128
T = 2048
E = 512
D = 32
H = E // D
QKV = E + 2 * D
KE = E // P
TILES = T // P
QB = 512
NQB = T // QB
UT = QB // P
HG = P // D
NG = NQB * H // HG
KC = T // P
KB = T // QB
QROWS = 3 * D
MROW = QROWS
AROWS = QROWS + 2
SCALE = float(D) ** -0.5
EPS = 1e-5

PV_LAG = 4
PRING = 8
MAXUNITS = HG * UT * KB
MAX_PLAN = [0, 2, 6, 6, 3, 3, 6, 6, 6, 6, 6, 6, 6, 2, 0, 0]
assert sum(MAX_PLAN) == MAXUNITS and len(MAX_PLAN) == KC
TAKE_STEP = PV_LAG
FILLS = 3 * HG


def build(nc, x, w_qkv_t, w_out_t, w_ffn_t, ffn_scale, ffn_bias, cos, sin, eye, out):
    x_t = x.rearrange("b (t p) e -> p (b t) e", p=P)
    out_t = out.rearrange("b (t p) e -> p (b t) e", p=P)

    with ExitStack() as ctx:
        def sb(name, shape, dt=F32):
            return ctx.enter_context(nc.sbuf_tensor(name, shape, dt))

        def psum(name, shape):
            return ctx.enter_context(nc.psum_tensor(name, shape, F32))

        def sem(name):
            return ctx.enter_context(nc.semaphore(name))

        wout = sb("wout", [P, KE, E])
        wffn = sb("wffn", [P, KE, E])
        bias_b = sb("bias_b", [P, E])
        scale_b = sb("scale_b", [P, E])
        cos_sb = sb("cos_sb", [P, TILES, D])
        sin_sb = sb("sin_sb", [P, TILES, D])
        ident = sb("ident", [P, P])
        ones = sb("ones", [P, D])
        eps = sb("eps", [P, 1])
        q_hi = sb("q_hi", [P, NG, QB])
        q_lo = sb("q_lo", [P, NG, QB])
        att = q_hi
        k_op = sb("k_op", [AROWS, T], F32R)
        q_op = sb("q_op", [AROWS, 2, HG, QB], F32R)
        v_sb = sb("v_sb", [P, KC, D])
        probs = sb("probs", [P, PRING, HG * QB])
        pair_sum = sb("pair_sum", [P, 2, HG * QB])
        wqkv = pair_sum[:].rearrange("p b n -> p (b n)")[:, 0:KE * QKV].rearrange("p (k n) -> p k n", k=KE)
        max_part = sb("max_part", [P, HG * UT, KB])
        neg_max = sb("neg_max", [P, HG * UT])
        nm_hi = sb("nm_hi", [HG * UT, P], F32R)
        nm_lo = sb("nm_lo", [HG * UT, P], F32R)
        o_sb = sb("o_sb", [P, QB])
        den_sb = sb("den_sb", [P, QB])
        rden = sb("rden", [P, QB])

        def room(slot, n, size=E):
            return probs[:, slot, 0:n * size].rearrange("p (n e) -> p n e", n=n)

        x_in = [room(0, 4), room(1, 4)]
        xln = room(2, 4)
        xT = room(3, 2)
        q_rot = probs[:, 3, 2 * E:4 * E].rearrange("p (n e) -> p n e", n=2)
        rot_a = room(4, 1, E + D)[:, 0, :]
        rot_b = probs[:, 4, 1024:1024 + E + D]
        k3 = probs[:, 5, 0:2 * QROWS].rearrange("p (n e) -> p n e", n=2)
        xe_in = room(0, 4)
        x1 = room(1, 4)
        yn = probs[:, 2, 0:2 * E].rearrange("p (n e) -> p n e", n=2)
        xl2 = probs[:, 2, 2 * E:4 * E].rearrange("p (n e) -> p n e", n=2)
        x2T = probs[:, 3, 0:2 * E].rearrange("p (n e) -> p n e", n=2)
        zb = probs[:, 3, 2 * E:4 * E].rearrange("p (n e) -> p n e", n=2)
        att_t = room(4, 4)
        zn = probs[:, 5, 0:2 * E].rearrange("p (n e) -> p n e", n=2)
        o_t = probs[:, 5, 2 * E:4 * E].rearrange("p (n e) -> p n e", n=2)

        st_a = sb("st_a", [P, 4, 6])
        mv_a = sb("mv_a", [P, 4, 2])
        sd_a = sb("sd_a", [P, 4])
        rs_a = sb("rs_a", [P, 4])
        st_e = sb("st_e", [P, 3, 6])
        mv_e = sb("mv_e", [P, 3, 2, 2])
        sd_e = sb("sd_e", [P, 3, 2])
        rs_e = sb("rs_e", [P, 3, 2])
        nm_e = sb("nm_e", [P, 2])

        s_ps = psum("s_ps", [P, 2, 2 * QB])
        mx_ps = psum("mx_ps", [P, 2, QB])
        o_ps = psum("o_ps", [P, QB])
        den_ps = psum("den_ps", [P, QB])

        w_loaded = sem("w_loaded")
        t_loaded = sem("t_loaded")
        e_loaded = sem("e_loaded")
        x_loaded = [sem("x_loaded0"), sem("x_loaded1")]
        const_set = sem("const_set")
        scaled = sem("scaled")
        dve_step = sem("dve_step")
        stats_a = sem("stats_a")
        std_a = sem("std_a")
        normed = sem("normed")
        x_turned = sem("x_turned")
        xT_ready = sem("xT_ready")
        qkv_done = sem("qkv_done")
        v_taken = sem("v_taken")
        rotated = sem("rotated")
        q_turned = sem("q_turned")
        hi_taken = sem("hi_taken")
        lo_taken = sem("lo_taken")

        q_filled = [sem("q_filled0"), sem("q_filled1")]
        mx_done = sem("mx_done")
        mx_reduced = sem("mx_reduced")
        neg_ready = sem("neg_ready")
        neg_turned = sem("neg_turned")
        neg_split = sem("neg_split")
        m_filled = sem("m_filled")
        qk_done = sem("qk_done")
        exp_done = sem("exp_done")
        pv_done = sem("pv_done")
        pairs_summed = sem("pairs_summed")
        den_done = sem("den_done")
        o_taken = sem("o_taken")
        den_taken = sem("den_taken")
        den_inv = sem("den_inv")
        att_ready = sem("att_ready")

        xe_loaded = [sem(f"xe_loaded{i}") for i in range(4)]
        att_loaded = [sem(f"att_loaded{i}") for i in range(4)]
        y_done = sem("y_done")
        y_stat = sem("y_stat")
        y_std = sem("y_std")
        y_inv = sem("y_inv")
        y_coef = sem("y_coef")
        y_normed = sem("y_normed")
        x1_ready = sem("x1_ready")
        x1_stat = sem("x1_stat")
        x1_std = sem("x1_std")
        x1_coef = sem("x1_coef")
        xl2_ready = sem("xl2_ready")
        x2_turned = sem("x2_turned")
        x2T_ready = sem("x2T_ready")
        z_done = sem("z_done")
        z_biased = sem("z_biased")
        z_stat = sem("z_stat")
        z_std = sem("z_std")
        z_coef = sem("z_coef")
        zn_ready = sem("zn_ready")
        o_ready = sem("o_ready")
        stored = [sem("stored0"), sem("stored1")]

        def wait(eng, s, n):
            if not isinstance(n, int) or n > 0:
                eng.wait_ge(s, n)

        def span(eng, first, last, end, body):
            for i in range(first):
                body(i)
            with eng.Fori(first, end - last) as i:
                body(i)
            for i in range(end - last, end):
                body(i)

        PAIRS = NG // 2
        SLOT_CHUNKS = NQB + 1

        def has(tile):
            return not isinstance(tile, int) or 0 <= tile < TILES

        block = ctx.enter_context(nc.Block())

        @block.sync
        def _(sp):
            def load_x(j):
                wait(sp, normed, 4 * (j - 1))
                sp.dma_start(x_in[j % 2], x_t[:, 4 * j:4 * j + 4, :]).then_inc(x_loaded[j % 2], 16)

            sp.dma_start(ident[:], eye).then_inc(t_loaded, 16)
            load_x(0)
            sp.dma_start(wqkv, w_qkv_t.rearrange("(k p) n -> p k n", p=P)).then_inc(w_loaded, 16)
            sp.dma_start(cos_sb[:], cos).then_inc(t_loaded, 16)
            sp.dma_start(sin_sb[:], sin).then_inc(t_loaded, 16)
            load_x(1)
            sp.dma_start(wout[:], w_out_t.rearrange("(k p) n -> p k n", p=P)).then_inc(e_loaded, 16)
            sp.dma_start(wffn[:], w_ffn_t.rearrange("(k p) n -> p k n", p=P)).then_inc(e_loaded, 16)
            sp.dma_start(scale_b[:], ffn_scale.partition_broadcast(P)).then_inc(e_loaded, 16)
            sp.dma_start(bias_b[:], ffn_bias.partition_broadcast(P)).then_inc(e_loaded, 16)
            load_x(2)
            load_x(3)

            def fill(g, b):
                for h in range(HG):
                    rows = slice(h * D, (h + 1) * D)
                    for at, part in enumerate((q_hi, q_hi, q_lo)):
                        sp.dma_start(q_op[at * D:(at + 1) * D, b, h, :].bitcast(F32),
                                     part[rows, bass.ds(g, 1), :]).then_inc(q_filled[b], 16)

            def fill_max(g, b):
                wait(sp, neg_split, 2 * (g + 1))
                for at, part in enumerate((nm_hi, nm_lo)):
                    sp.dma_start(q_op[MROW + at:MROW + at + 1, b, :, :].rearrange("r h (u q) -> r (h u) q", u=UT)
                                 .bitcast(F32), part[:].bitcast(F32)).then_inc(m_filled, 16)

            sp.wait_ge(hi_taken, 2 * TILES)
            sp.wait_ge(lo_taken, 2 * TILES)
            fill(0, 0)
            fill_max(0, 0)

            def turn(j):
                for b in range(2):
                    g = 2 * j + b
                    if isinstance(g, int) and g + 1 == NG:
                        break
                    wait(sp, qk_done, 2 * KC * g)
                    fill(g + 1, 1 - b)
                    fill_max(g + 1, 1 - b)

            span(sp, 1, 1, PAIRS, turn)

            sp.wait_ge(att_ready, NG)
            sp.wait_ge(pv_done, NG * KC)
            sp.wait_ge(pairs_summed, NG * KC // 2)

            def slots(j):
                for u in range(4):
                    s = 4 * j + u
                    if has(s):
                        wait(sp, x1_ready, s - 3)
                        wait(sp, y_done, s - 3)
                        sp.dma_start(xe_in[:, u, :], x_t[:, bass.ds(s, 1), :]).then_inc(xe_loaded[u], 16)
                        src = att[:, bass.ds(4 * j, 4), u * P:(u + 1) * P]
                        sp.dma_start(att_t[:, u, :].rearrange("p (q n) -> p q n", q=KE), src).then_inc(att_loaded[u], 16)
                    if has(s - 4):
                        sp.wait_ge(o_ready, s - 3)
                        sp.dma_start(out_t[:, bass.ds(s - 4, 1), :], o_t[:, u % 2, :]).then_inc(stored[u % 2], 16)

            span(sp, 1, 1, SLOT_CHUNKS, slots)
            for s in stored:
                sp.wait_ge(s, 16 * TILES // 2)

        @block.gpsimd
        def _(pool):
            nc.gpsimd.memset(ones[:], 1.0).then_inc(const_set, 1)
            nc.gpsimd.memset(eps[:], EPS).then_inc(const_set, 1)
            pool.wait_ge(const_set, 2)
            nc.gpsimd.memset(k_op[MROW:MROW + 2, :].bitcast(F32), 1.0).then_inc(const_set, 1)
            pool.wait_ge(e_loaded, 64)
            pool.wait_ge(const_set, 3)
            for k in range(KE):
                nc.gpsimd.tensor_tensor(wffn[:, k, :], wffn[:, k, :], scale_b[:], ALU.mult).then_inc(scaled, 1)

            def turn(j):
                for i in range(KC):
                    n = j * KC + i
                    wait(pool, exp_done, 4 * n + 4)
                    wait(pool, den_done, n - 1)
                    c = 2 * i % PRING
                    nc.gpsimd.tensor_tensor(pair_sum[:, i % 2, :], probs[:, c, :], probs[:, c + 1, :],
                                            ALU.add).then_inc(pairs_summed, 1)

            span(pool, 1, 1, PAIRS, turn)

            def slots(j):
                for u in range(4):
                    s = 4 * j + u
                    if has(s - 1):
                        t, r = s - 1, (u - 1) % 4
                        pool.wait_ge(y_normed, t + 1)
                        pool.wait_ge(xe_loaded[r], 16 * ((j if r < 3 else j - 1) + 1))
                        wait(pool, xl2_ready, t - 3)
                        wait(pool, o_ready, t - 3)
                        nc.gpsimd.tensor_tensor(x1[:, r, :], xe_in[:, r, :], yn[:, (u - 1) % 2, :],
                                                ALU.add).then_inc(x1_ready, 1)
                    if has(s - 4):
                        pool.wait_ge(zn_ready, s - 3)
                        wait(pool, stored[u % 2], 16 * (2 * j - 2 + u // 2))
                        nc.gpsimd.tensor_tensor(o_t[:, u % 2, :], x1[:, u, :], zn[:, u % 2, :],
                                                ALU.add).then_inc(o_ready, 1)

            span(pool, 1, 1, SLOT_CHUNKS, slots)

        @block.scalar
        def _(act):
            act.wait_ge(const_set, 3)

            def chunk(j):
                act.wait_ge(stats_a, j + 1)
                nc.scalar.activation(sd_a[:], mv_a[:, :, 1], ACT.Sqrt, bias=eps[:, 0:1]).then_inc(std_a, 1)

                def take_xT(u):
                    t = 4 * j + u
                    act.wait_ge(x_turned, t + 1)
                    wait(act, qkv_done, t - 1)
                    nc.scalar.activation(xT[:, u % 2, :], mx_ps[:, u % 2, :], ACT.Copy).then_inc(xT_ready, 1)

                def take_v(u):
                    t = 4 * j + u
                    act.wait_ge(qkv_done, t + 1)
                    nc.scalar.activation(v_sb[:, bass.ds(t, 1), :],
                                         s_ps[:, u % 2, E + D:QKV].unsqueeze(1), ACT.Copy).then_inc(v_taken, 1)

                def take_hi(u):
                    t = 4 * j + u
                    act.wait_ge(q_turned, t + 1)
                    nc.scalar.activation(q_hi[:, bass.ds(4 * j, 4), u * P:(u + 1) * P].bitcast(F32R),
                                         o_ps[:].rearrange("p (q n) -> p q n", q=KE), ACT.Copy).then_inc(hi_taken, 1)
                    nc.scalar.activation(k_op[0:QROWS, bass.ds(t * P, P)],
                                         den_ps[0:QROWS, 0:P], ACT.Copy).then_inc(hi_taken, 1)

                take_xT(0)
                take_xT(1)
                take_v(0)
                take_xT(2)
                take_v(1)
                take_hi(0)
                take_xT(3)
                take_v(2)
                take_hi(1)
                take_v(3)
                take_hi(2)
                take_hi(3)

            span(act, 1, 0, NQB, chunk)
            act.wait_ge(lo_taken, 2 * TILES)
            act.wait_ge(q_turned, TILES)

            def turn(j):
                for i in range(2 * KC):
                    b, c = divmod(i, KC)
                    if c == TAKE_STEP and not (isinstance(j, int) and j == 0 and b == 0):
                        act.wait_ge(den_done, (2 * j + b) * KC // 2)
                        wait(act, den_inv, 2 * j + b - 1)
                        nc.scalar.activation(den_sb[:], den_ps[:], ACT.Copy).then_inc(den_taken, 1)
                    n = j * 2 * KC + i
                    for p in range(2):
                        act.wait_ge(qk_done, 2 * n + p + 1)
                        if p == 0:
                            wait(act, pv_done, n - PRING + 1)
                            wait(act, pairs_summed, j * KC + (i // 2 - PRING // 2 + 1))
                        nc.scalar.activation(probs[:, i % PRING, p * 2 * QB:(p + 1) * 2 * QB], s_ps[:, p, :],
                                             ACT.Exp, scale=SCALE).then_inc(exp_done, 1)

            span(act, 1, 1, PAIRS, turn)
            act.wait_ge(den_done, NG * KC // 2)
            act.wait_ge(den_inv, NG - 1)
            nc.scalar.activation(den_sb[:], den_ps[:], ACT.Copy).then_inc(den_taken, 1)

            def std(stat, done, k, t, r):
                act.wait_ge(stat, t + 1)
                nc.scalar.activation(sd_e[:, k, r:r + 1], mv_e[:, k, r, 1:2], ACT.Sqrt,
                                     bias=eps[:, 0:1]).then_inc(done, 1)

            def slots(j):
                for u in range(4):
                    s = 4 * j + u
                    if has(s - 1):
                        std(y_stat, y_std, 0, s - 1, (u - 1) % 2)
                    if has(s - 2):
                        std(x1_stat, x1_std, 1, s - 2, u % 2)
                    if has(s - 3):
                        act.wait_ge(x2_turned, s - 2)
                        wait(act, z_done, s - 4)
                        nc.scalar.activation(x2T[:, (u - 3) % 2, :], mx_ps[:, (u - 3) % 2, :],
                                             ACT.Copy).then_inc(x2T_ready, 1)
                    if has(s - 4):
                        std(z_stat, z_std, 2, s - 4, u % 2)
                    if has(s - 1):
                        act.wait_ge(y_coef, s)
                        wait(act, x1_ready, s - 2)
                        nc.scalar.activation(yn[:, (u - 1) % 2, :], s_ps[:, (u - 1) % 2, 0:E], ACT.Identity,
                                             bias=nm_e[:, (u - 1) % 2:(u - 1) % 2 + 1],
                                             scale=rs_e[:, 0, (u - 1) % 2:(u - 1) % 2 + 1]).then_inc(y_normed, 1)

            span(act, 1, 1, SLOT_CHUNKS, slots)

        @block.vector
        def _(dve):
            dve.wait_ge(t_loaded, 48)

            CHUNK_STEPS = 3 + 1 + 4 * 4

            def chunk_pair(i):
                for b in range(2):
                    j = 2 * i + b
                    own = [CHUNK_STEPS * j]

                    def step(ins):
                        own[0] = own[0] + 1
                        ins.then_inc(dve_step, 1)

                    def settle():
                        dve.wait_ge(dve_step, own[0])

                    dve.wait_ge(x_loaded[b], 16 * (i + 1))
                    for u in range(4):
                        nc.vector.bn_stats(st_a[:, u, :], x_in[b][:, u, :])
                    nc.vector.drain()
                    for u in range(4):
                        ins = nc.vector.bn_aggr(mv_a[:, u, :], st_a[:, u, :])
                        if u < 3:
                            step(ins)
                        else:
                            ins.then_inc(stats_a, 1)
                    dve.wait_ge(std_a, j + 1)
                    step(nc.vector.reciprocal(rs_a[:], sd_a[:]))
                    settle()
                    for u in range(4):
                        wait(dve, x_turned, 4 * j + u - 3)
                        nc.vector.tensor_scalar(xln[:, u, :], x_in[b][:, u, :], mv_a[:, u, 0:1], rs_a[:, u:u + 1],
                                                ALU.subtract, ALU.mult).then_inc(normed, 1)

                    def rotate(u):
                        t = 4 * j + u
                        n = H + 1
                        src = s_ps[:, u % 2, 0:E + D].rearrange("p (h two d) -> p h two d", two=2, d=D // 2)
                        ra = rot_a.rearrange("p (h d) -> p h d", d=D)
                        rb = rot_b.rearrange("p (h two d) -> p h two d", two=2, d=D // 2)
                        cs = cos_sb[:, bass.ds(t, 1), :].to_broadcast([P, n, D])
                        sn = sin_sb[:, bass.ds(t, 1), :]
                        dve.wait_ge(qkv_done, t + 1)
                        dve.wait_ge(v_taken, t + 1)
                        settle()
                        step(nc.vector.tensor_tensor(
                            ra, s_ps[:, u % 2, 0:E + D].rearrange("p (h d) -> p h d", d=D), cs, ALU.mult))
                        for half in range(2):
                            step(nc.vector.tensor_tensor(
                                rb[:, :, half, :], src[:, :, 1 - half, :],
                                sn[:, :, half * D // 2:(half + 1) * D // 2].to_broadcast([P, n, D // 2]), ALU.mult))
                        settle()
                        wait(dve, q_turned, t - 1)
                        step(nc.vector.tensor_tensor(q_rot[:, u % 2, :], rot_a[:, 0:E], rot_b[:, 0:E], ALU.add))
                        nc.vector.tensor_tensor(k3[:, u % 2, :].rearrange("p (n d) -> p n d", n=3),
                                                rot_a[:, E:E + D].unsqueeze(1).to_broadcast([P, 3, D]),
                                                rot_b[:, E:E + D].unsqueeze(1).to_broadcast([P, 3, D]),
                                                ALU.add).then_inc(rotated, 1)
                        settle()
                        dve.wait_ge(rotated, t + 1)

                    def take_lo(u):
                        t = 4 * j + u
                        dve.wait_ge(hi_taken, 2 * t + 2)
                        at = (slice(None), bass.ds(4 * j, 4), slice(u * P, (u + 1) * P))
                        nc.vector.tensor_tensor(q_lo[at].bitcast(F32R), o_ps[:].rearrange("p (q n) -> p q n", q=KE),
                                                q_hi[at], ALU.subtract).then_inc(lo_taken, 1)
                        kl = k_op[D:2 * D, bass.ds(t * P, P)]
                        nc.vector.tensor_tensor(kl, den_ps[D:2 * D, 0:P], kl.bitcast(F32),
                                                ALU.subtract).then_inc(lo_taken, 1)

                    rotate(0)
                    rotate(1)
                    rotate(2)
                    take_lo(0)
                    rotate(3)
                    take_lo(1)
                    take_lo(2)
                    take_lo(3)

            span(dve, 1, 0, NQB // 2, chunk_pair)

            def reduce_units(g, first, count):
                for k in range(first, first + count):
                    n = g * MAXUNITS + k
                    dve.wait_ge(mx_done, n + 1)
                    nc.vector.tensor_reduce(max_part[:, k // KB, k % KB:k % KB + 1], mx_ps[:, k % 2, :], AX.X,
                                            ALU.max).then_inc(mx_reduced, 1)

            def negate(g):
                dve.wait_ge(mx_reduced, (g + 1) * MAXUNITS)
                wait(dve, neg_turned, g)
                nc.vector.tensor_reduce(neg_max[:], max_part[:], AX.X, ALU.max, negate=True).then_inc(neg_ready, 1)

            def split(g):
                dve.wait_ge(neg_turned, g + 1)
                wait(dve, m_filled, 32 * g)
                turned = mx_ps[0:HG * UT, 0, 0:P]
                nc.vector.tensor_copy(nm_hi[:], turned).then_inc(neg_split, 1)
                dve.wait_ge(neg_split, 2 * g + 1)
                nc.vector.tensor_tensor(nm_lo[:], turned, nm_hi[:].bitcast(F32), ALU.subtract).then_inc(neg_split, 1)

            def take(g):
                dve.wait_ge(pv_done, (g + 1) * KC)
                wait(dve, att_ready, g)
                nc.vector.tensor_copy(o_sb[:], o_ps[:]).then_inc(o_taken, 1)

            def invert(g):
                dve.wait_ge(den_taken, g + 1)
                wait(dve, att_ready, g)
                nc.vector.reciprocal(rden[:], den_sb[:]).then_inc(den_inv, 1)

            def finish(g):
                dve.wait_ge(den_inv, g + 1)
                dve.wait_ge(o_taken, g + 1)
                nc.vector.tensor_tensor(att[:, bass.ds(g, 1), :], o_sb[:].unsqueeze(1), rden[:].unsqueeze(1),
                                        ALU.mult).then_inc(att_ready, 1)

            reduce_units(0, 0, MAXUNITS)
            negate(0)
            split(0)

            def turn(j):
                for b in range(2):
                    g = 2 * j + b
                    more = not (isinstance(g, int) and g + 1 == NG)
                    before = not (isinstance(g, int) and g == 0)
                    first = 0
                    for c in range(KC):
                        if c == TAKE_STEP and before:
                            take(g - 1)
                        if more:
                            reduce_units(g + 1, first, MAX_PLAN[c])
                            first += MAX_PLAN[c]
                            if MAX_PLAN[c] and first == MAXUNITS:
                                negate(g + 1)
                                split(g + 1)
                        if c == TAKE_STEP and before:
                            invert(g - 1)
                        if c == TAKE_STEP + 1 and before:
                            finish(g - 1)

            span(dve, 1, 1, PAIRS, turn)
            take(NG - 1)
            invert(NG - 1)
            finish(NG - 1)

            def stats(src, k, r, stat, t):
                nc.vector.bn_stats(st_e[:, k, :], src)
                nc.vector.drain()
                nc.vector.bn_aggr(mv_e[:, k, r, :], st_e[:, k, :]).then_inc(stat, 1)

            def coef(k, r, done, coefs, t):
                dve.wait_ge(done, t + 1)
                nc.vector.reciprocal(rs_e[:, k, r:r + 1], sd_e[:, k, r:r + 1]).then_inc(coefs, 1)

            def slots(j):
                for u in range(4):
                    s = 4 * j + u
                    if has(s - 1):
                        t, r = s - 1, (u - 1) % 2
                        dve.wait_ge(y_done, t + 1)
                        wait(dve, y_normed, t - 1)
                        stats(s_ps[:, r, 0:E], 0, r, y_stat, t)
                    if has(s - 2):
                        t, r = s - 2, u % 2
                        dve.wait_ge(x1_ready, t + 1)
                        wait(dve, xl2_ready, t - 1)
                        stats(x1[:, (u - 2) % 4, :], 1, r, x1_stat, t)
                    if has(s - 4):
                        t, r = s - 4, u % 2
                        dve.wait_ge(z_done, t + 1)
                        wait(dve, zn_ready, t)
                        nc.vector.tensor_tensor(zb[:, r, :], s_ps[:, r, E:2 * E], bias_b[:], ALU.add).then_inc(z_biased, 1)
                        dve.wait_ge(z_biased, t + 1)
                        stats(zb[:, r, :], 2, r, z_stat, t)
                    if has(s - 1):
                        t, r = s - 1, (u - 1) % 2
                        dve.wait_ge(y_std, t + 1)
                        nc.vector.reciprocal(rs_e[:, 0, r:r + 1], sd_e[:, 0, r:r + 1]).then_inc(y_inv, 1)
                        dve.wait_ge(y_inv, t + 1)
                        nc.vector.tensor_scalar(nm_e[:, r:r + 1], mv_e[:, 0, r, 0:1], rs_e[:, 0, r:r + 1], -1.0,
                                                ALU.mult, ALU.mult).then_inc(y_coef, 1)
                    if has(s - 2):
                        t, r = s - 2, u % 2
                        coef(1, r, x1_std, x1_coef, t)
                        dve.wait_ge(x1_coef, t + 1)
                        wait(dve, x2_turned, t - 1)
                        nc.vector.tensor_scalar(xl2[:, r, :], x1[:, (u - 2) % 4, :], mv_e[:, 1, r, 0:1],
                                                rs_e[:, 1, r:r + 1], ALU.subtract, ALU.mult).then_inc(xl2_ready, 1)
                    if has(s - 4):
                        t, r = s - 4, u % 2
                        coef(2, r, z_std, z_coef, t)
                        dve.wait_ge(z_coef, t + 1)
                        wait(dve, o_ready, t)
                        nc.vector.tensor_scalar(zn[:, r, :], zb[:, r, :], mv_e[:, 2, r, 0:1],
                                                rs_e[:, 2, r:r + 1], ALU.subtract, ALU.mult).then_inc(zn_ready, 1)

            span(dve, 1, 1, SLOT_CHUNKS, slots)

        @block.tensor
        def _(pe):
            def turn_tile(dst, src):
                for k in range(KE):
                    last = nc.tensor.transpose(dst[:, k * P:(k + 1) * P], src[:, k * P:(k + 1) * P], ident[:])
                return last

            pe.wait_ge(t_loaded, 48)
            pe.wait_ge(w_loaded, 16)

            def chunk(j):
                def turn_x(u):
                    t = 4 * j + u
                    pe.wait_ge(normed, t + 1)
                    wait(pe, xT_ready, t - 1)
                    turn_tile(mx_ps[:, u % 2, :], xln[:, u, :]).then_inc(x_turned, 1)

                def project(u):
                    t = 4 * j + u
                    pe.wait_ge(xT_ready, t + 1)
                    wait(pe, rotated, t - 1)
                    wait(pe, v_taken, t - 1)
                    for cols in (slice(0, E), slice(E, QKV)):
                        for k in range(KE):
                            last = nc.tensor.matmul(s_ps[:, u % 2, cols], xT[:, u % 2, k * P:(k + 1) * P],
                                                    wqkv[:, k, cols], start=(k == 0), stop=(k == KE - 1))
                    last.then_inc(qkv_done, 1)

                def turn_qk(u):
                    t = 4 * j + u
                    pe.wait_ge(rotated, t + 1)
                    wait(pe, lo_taken, 2 * t)
                    turn_tile(o_ps[:], q_rot[:, u % 2, :])
                    nc.tensor.transpose(den_ps[0:QROWS, 0:P], k3[:, u % 2, :], ident[:]).then_inc(q_turned, 1)

                turn_x(0)
                turn_x(1)
                project(0)
                turn_x(2)
                project(1)
                turn_qk(0)
                turn_x(3)
                project(2)
                turn_qk(1)
                project(3)
                turn_qk(2)
                turn_qk(3)

            span(pe, 1, 0, NQB, chunk)

            def max_units(g, b, first, count):
                for k in range(first, first + count):
                    h, u, kb = k // (UT * KB), k // KB % UT, k % KB
                    n = g * MAXUNITS + k
                    wait(pe, mx_reduced, n - 1)
                    nc.tensor.matmul(mx_ps[:, k % 2, :], q_op[0:QROWS, b, h, u * P:(u + 1) * P],
                                     k_op[0:QROWS, kb * QB:(kb + 1) * QB], start=True, stop=True).then_inc(mx_done, 1)

            def turn_max(g):
                pe.wait_ge(neg_ready, g + 1)
                nc.tensor.transpose(mx_ps[0:HG * UT, 0, 0:P], neg_max[:], ident[:]).then_inc(neg_turned, 1)

            def scores(n, b, c, p):
                wait(pe, exp_done, 2 * n + p - 1)
                for h in (2 * p, 2 * p + 1):
                    last = nc.tensor.matmul(s_ps[:, p, (h % 2) * QB:(h % 2 + 1) * QB], k_op[:, c * P:(c + 1) * P],
                                            q_op[:, b, h, :], start=True, stop=True)
                last.then_inc(qk_done, 1)

            def weighted_sum(n, c):
                pe.wait_ge(exp_done, 2 * n + 2)
                for h in range(HG):
                    last = nc.tensor.matmul(o_ps[h * D:(h + 1) * D, :], v_sb[:, c, :],
                                            probs[:, c % PRING, h * QB:(h + 1) * QB],
                                            start=(c == 0), stop=(c == KC - 1))
                last.then_inc(pv_done, 1)

            def total(n, i):
                pe.wait_ge(pairs_summed, n + 1)
                for h in range(HG):
                    last = nc.tensor.matmul(den_ps[h * D:(h + 1) * D, :], ones[:],
                                            pair_sum[:, i % 2, h * QB:(h + 1) * QB],
                                            start=(i == 0), stop=(i == KC // 2 - 1))
                last.then_inc(den_done, 1)

            def lagged(g, c):
                if c == 0:
                    wait(pe, o_taken, g)
                    wait(pe, den_taken, g)
                weighted_sum(g * KC + c, c)
                if c % 2:
                    total(g * (KC // 2) + c // 2, c // 2)

            pe.wait_ge(const_set, 3)
            pe.wait_ge(lo_taken, 2 * TILES)
            pe.wait_ge(hi_taken, 2 * TILES)
            pe.wait_ge(q_filled[0], 16 * FILLS)
            max_units(0, 0, 0, MAXUNITS)
            turn_max(0)

            def turn(j):
                for b in range(2):
                    g = 2 * j + b
                    more = not (isinstance(g, int) and g + 1 == NG)
                    first = 0
                    pe.wait_ge(m_filled, 32 * (g + 1))
                    for c in range(KC):
                        scores(g * KC + c, b, c, 0)
                        count = MAX_PLAN[c] if more else 0
                        if count and first == 0:
                            pe.wait_ge(q_filled[1 - b], 16 * FILLS * (j + 1 + b))
                            pe.wait_ge(neg_split, 2 * (g + 1))
                        max_units(g + 1, 1 - b, first, count // 2)
                        scores(g * KC + c, b, c, 1)
                        max_units(g + 1, 1 - b, first + count // 2, count - count // 2)
                        first += count
                        if count and first == MAXUNITS:
                            turn_max(g + 1)
                        if c >= PV_LAG:
                            lagged(g, c - PV_LAG)
                        elif not (isinstance(g, int) and g == 0):
                            lagged(g - 1, KC + c - PV_LAG)

            span(pe, 1, 1, PAIRS, turn)
            for c in range(KC - PV_LAG, KC):
                lagged(NG - 1, c)

            pe.wait_ge(scaled, KE)
            pe.wait_ge(e_loaded, 64)

            def slots(j):
                for u in range(4):
                    s = 4 * j + u
                    if has(s - 3):
                        t = s - 3
                        pe.wait_ge(xl2_ready, t + 1)
                        wait(pe, x2T_ready, t - 1)
                        turn_tile(mx_ps[:, (u - 3) % 2, :], xl2[:, (u - 3) % 2, :]).then_inc(x2_turned, 1)
                    if has(s):
                        pe.wait_ge(att_loaded[u], 16 * (j + 1))
                        wait(pe, y_normed, s - 1)
                        for k in range(KE):
                            last = nc.tensor.matmul(s_ps[:, u % 2, 0:E], att_t[:, u, k * P:(k + 1) * P],
                                                    wout[:, k, :], start=(k == 0), stop=(k == KE - 1))
                        last.then_inc(y_done, 1)
                    if has(s - 3):
                        t, r = s - 3, (u - 3) % 2
                        pe.wait_ge(x2T_ready, t + 1)
                        wait(pe, z_biased, t - 1)
                        for k in range(KE):
                            last = nc.tensor.matmul(s_ps[:, r, E:2 * E], x2T[:, r, k * P:(k + 1) * P],
                                                    wffn[:, k, :], start=(k == 0), stop=(k == KE - 1))
                        last.then_inc(z_done, 1)

            span(pe, 1, 1, SLOT_CHUNKS, slots)


def kernel(**inputs):
    import numpy as np
    import concourse.bacc as bacc
    from concourse.bass_utils import run_bass_kernel_spmd

    pos = (10000.0 ** ((-2.0 * np.arange(0, D, 2) - 1.0) / D)).astype(np.float32)
    angles = np.arange(T, dtype=np.float32)[:, None] * pos[None, :]
    cos = np.concatenate([np.cos(angles), np.cos(angles)], axis=1)
    sin = np.concatenate([-np.sin(angles), np.sin(angles)], axis=1)

    def by_tile(a):
        return np.ascontiguousarray(a.reshape(TILES, P, D).transpose(1, 0, 2))

    arrays = {
        "x": np.ascontiguousarray(inputs["L0_attn_x"]),
        "w_qkv_t": np.ascontiguousarray(np.asarray(inputs["L0_attn_w_attn"]).T),
        "w_out_t": np.ascontiguousarray(np.asarray(inputs["L0_attn_w_out"]).T),
        "w_ffn_t": np.ascontiguousarray(np.asarray(inputs["L0_ffn_weight"]).T),
        "ffn_scale": np.ascontiguousarray(inputs["L0_ffn_scale_weight"]),
        "ffn_bias": np.ascontiguousarray(inputs["L0_ffn_bias"]),
        "cos": by_tile(cos),
        "sin": by_tile(sin),
        "eye": np.eye(P, dtype=np.float32),
    }
    nc = bacc.Bacc("TRN2", target_bir_lowering=False, num_devices=1)
    args = [nc.dram_tensor(n, a.shape, mybir.dt.from_np(a.dtype), kind="ExternalInput").ap() for n, a in arrays.items()]
    out = nc.dram_tensor("out", (1, T, E), F32, kind="ExternalOutput").ap()
    build(nc, *args, out)
    r = run_bass_kernel_spmd(nc, [arrays], core_ids=[0])
    return r.results[0]["out"]
```

```python
from contextlib import ExitStack

import concourse.bass as bass
from concourse import mybir

F32 = mybir.dt.float32
F32R = mybir.dt.float32r
ALU = mybir.AluOpType
ACT = mybir.ActivationFunctionType
AX = mybir.AxisListType

P = 128
T = 2048
E = 512
D = 32
H = E // D
QKV = E + 2 * D
KE = E // P
TILES = T // P
QB = 512
NQB = T // QB
UT = QB // P
HG = P // D
NG = NQB * H // HG
KC = T // P
KB = T // QB
QROWS = 3 * D
MROW = QROWS
AROWS = QROWS + 2
SCALE = float(D) ** -0.5
EPS = 1e-5

PV_LAG = 4
PRING = 8
MAXUNITS = HG * UT * KB // 2
MAX_PLAN = [0, 1, 2, 4, 1, 3, 2, 4, 2, 4, 2, 4, 2, 1, 0, 0]
assert sum(MAX_PLAN) == MAXUNITS and len(MAX_PLAN) == KC
TAKE_STEP = PV_LAG
TURN_STEP = KC - 2
FILLS = 3


def build(nc, x, w_qkv_t, w_out_t, w_ffn_t, ffn_scale, ffn_bias, cos, sin, eye, out):
    x_t = x.rearrange("b (t p) e -> p (b t) e", p=P)
    out_t = out.rearrange("b (t p) e -> p (b t) e", p=P)

    with ExitStack() as ctx:
        def sb(name, shape, dt=F32):
            return ctx.enter_context(nc.sbuf_tensor(name, shape, dt))

        def psum(name, shape):
            return ctx.enter_context(nc.psum_tensor(name, shape, F32))

        def sem(name):
            return ctx.enter_context(nc.semaphore(name))

        wout = sb("wout", [P, KE, E])
        wffn = sb("wffn", [P, KE, E])
        bias_b = sb("bias_b", [P, E])
        scale_b = sb("scale_b", [P, E])
        cos_sb = sb("cos_sb", [P, TILES, D])
        sin_sb = sb("sin_sb", [P, TILES, D])
        ident = sb("ident", [P, P])
        ones = sb("ones", [P, D])
        eps = sb("eps", [P, 1])
        q_hi = sb("q_hi", [P, NG, QB])
        q_lo = sb("q_lo", [P, NG, QB])
        att = q_hi
        k_op = sb("k_op", [AROWS, T], F32R)
        q_op = sb("q_op", [AROWS, 2, HG, QB], F32R)
        v_sb = sb("v_sb", [P, KC, D])
        probs = sb("probs", [P, PRING, HG * QB])
        pair_sum = sb("pair_sum", [P, 2, HG * QB])
        wqkv = pair_sum[:].rearrange("p b n -> p (b n)")[:, 0:KE * QKV].rearrange("p (k n) -> p k n", k=KE)
        max_part = sb("max_part", [P, HG * UT, KB // 2])
        neg_max = sb("neg_max", [P, HG * UT])
        neg_parts = sb("neg_parts", [P, 2 * HG * UT])
        neg_t = sb("neg_t", [2 * HG * UT, P], F32R)
        o_sb = sb("o_sb", [P, QB])
        den_sb = sb("den_sb", [P, QB])
        rden = sb("rden", [P, QB])

        def room(slot, n, size=E):
            return probs[:, slot, 0:n * size].rearrange("p (n e) -> p n e", n=n)

        x_in = room(0, 4)
        xln = room(2, 4)
        xT = room(3, 2)
        q_rot = probs[:, 3, 2 * E:4 * E].rearrange("p (n e) -> p n e", n=2)
        rot_a = room(4, 1, E + D)[:, 0, :]
        rot_b = probs[:, 4, 1024:1024 + E + D]
        k3 = probs[:, 5, 0:2 * QROWS].rearrange("p (n e) -> p n e", n=2)
        xe_in = room(0, 4)
        x1 = room(1, 4)
        yn = probs[:, 2, 0:2 * E].rearrange("p (n e) -> p n e", n=2)
        xl2 = probs[:, 2, 2 * E:4 * E].rearrange("p (n e) -> p n e", n=2)
        x2T = probs[:, 3, 0:2 * E].rearrange("p (n e) -> p n e", n=2)
        zb = probs[:, 3, 2 * E:4 * E].rearrange("p (n e) -> p n e", n=2)
        att_t = room(4, 4)
        zn = probs[:, 5, 0:2 * E].rearrange("p (n e) -> p n e", n=2)
        o_t = probs[:, 5, 2 * E:4 * E].rearrange("p (n e) -> p n e", n=2)

        st_a = sb("st_a", [P, 4, 6])
        mv_a = sb("mv_a", [P, 4, 2])
        sd_a = sb("sd_a", [P, 4])
        rs_a = sb("rs_a", [P, 4])
        st_e = sb("st_e", [P, 3, 6])
        mv_e = sb("mv_e", [P, 3, 2, 2])
        sd_e = sb("sd_e", [P, 3, 2])
        rs_e = sb("rs_e", [P, 3, 2])
        nm_e = sb("nm_e", [P, 2])

        s_ps = psum("s_ps", [P, 2, QB])
        mx_ps = psum("mx_ps", [P, 2, 2 * QB])
        o_ps = psum("o_ps", [P, QB])
        den_ps = psum("den_ps", [P, QB])

        w_loaded = sem("w_loaded")
        t_loaded = sem("t_loaded")
        e_loaded = sem("e_loaded")
        x_loaded = [sem(f"x_loaded{u}") for u in range(4)]
        const_set = sem("const_set")
        scaled = sem("scaled")
        inverse_a = sem("inverse_a")
        products = sem("products")
        stats_a = sem("stats_a")
        std_a = sem("std_a")
        normed = sem("normed")
        x_turned = sem("x_turned")
        xT_ready = sem("xT_ready")
        qkv_done = sem("qkv_done")
        v_taken = sem("v_taken")
        rotated = sem("rotated")
        q_turned = sem("q_turned")
        hi_taken = sem("hi_taken")
        lo_taken = sem("lo_taken")

        q_filled = [[sem(f"q_filled{b}_{h}") for h in range(HG)] for b in range(2)]
        mx_done = sem("mx_done")
        mx_reduced = sem("mx_reduced")
        neg_ready = sem("neg_ready")
        neg_split = sem("neg_split")
        neg_turned = sem("neg_turned")
        neg_taken = sem("neg_taken")
        m_filled = sem("m_filled")
        qk_done = sem("qk_done")
        exp_done = sem("exp_done")
        pv_done = sem("pv_done")
        pairs_summed = sem("pairs_summed")
        den_done = sem("den_done")
        o_taken = sem("o_taken")
        den_taken = sem("den_taken")
        den_inv = sem("den_inv")
        att_ready = sem("att_ready")

        xe_loaded = [sem(f"xe_loaded{i}") for i in range(4)]
        att_loaded = [sem(f"att_loaded{i}") for i in range(4)]
        y_done = sem("y_done")
        y_stat = sem("y_stat")
        y_std = sem("y_std")
        y_inv = sem("y_inv")
        y_coef = sem("y_coef")
        y_normed = sem("y_normed")
        x1_ready = sem("x1_ready")
        x1_stat = sem("x1_stat")
        x1_std = sem("x1_std")
        x1_coef = sem("x1_coef")
        xl2_ready = sem("xl2_ready")
        x2_turned = sem("x2_turned")
        x2T_ready = sem("x2T_ready")
        z_done = sem("z_done")
        z_biased = sem("z_biased")
        z_stat = sem("z_stat")
        z_std = sem("z_std")
        z_coef = sem("z_coef")
        zn_ready = sem("zn_ready")
        o_ready = sem("o_ready")
        stored = [sem("stored0"), sem("stored1")]

        def wait(eng, s, n):
            if not isinstance(n, int) or n > 0:
                eng.wait_ge(s, n)

        def span(eng, first, last, end, body, start=0):
            first = max(first, start)
            for i in range(start, first):
                body(i)
            if end - last > first:
                with eng.Fori(first, end - last) as i:
                    body(i)
            for i in range(max(first, end - last), end):
                body(i)

        PAIRS = NG // 2
        SLOT_CHUNKS = NQB + 1

        def q_part(t, u):
            return (slice(None), bass.ds(t - u, HG), slice(u * P, (u + 1) * P))

        def has(tile):
            return not isinstance(tile, int) or 0 <= tile < TILES

        block = ctx.enter_context(nc.Block())

        @block.sync
        def _(sp):
            def load_x(t, u):
                sp.dma_start(x_in[:, u, :], x_t[:, bass.ds(t, 1), :]).then_inc(x_loaded[u], 16)

            for u in range(4):
                load_x(u, u)
            sp.dma_start(ident[:], eye).then_inc(t_loaded, 16)
            sp.dma_start(wqkv, w_qkv_t.rearrange("(k p) n -> p k n", p=P)).then_inc(w_loaded, 16)
            sp.dma_start(cos_sb[:], cos).then_inc(t_loaded, 16)
            sp.dma_start(sin_sb[:], sin).then_inc(t_loaded, 16)

            def reload(j):
                for u in range(4):
                    sp.wait_ge(normed, 4 * j + u - 3)
                    load_x(4 * j + u, u)

            span(sp, 2, 0, NQB, reload, start=1)
            sp.dma_start(wout[:], w_out_t.rearrange("(k p) n -> p k n", p=P)).then_inc(e_loaded, 16)
            sp.dma_start(wffn[:], w_ffn_t.rearrange("(k p) n -> p k n", p=P)).then_inc(e_loaded, 16)
            sp.dma_start(scale_b[:], ffn_scale.partition_broadcast(P)).then_inc(e_loaded, 16)
            sp.dma_start(bias_b[:], ffn_bias.partition_broadcast(P)).then_inc(e_loaded, 16)

            def fill(g, b):
                for h in range(HG):
                    rows = slice(h * D, (h + 1) * D)
                    for at, part in enumerate((q_hi, q_hi, q_lo)):
                        sp.dma_start(q_op[at * D:(at + 1) * D, b, h, :].bitcast(F32),
                                     part[rows, bass.ds(g, 1), :]).then_inc(q_filled[b][h], 16)

            def fill_max(g, b):
                sp.wait_ge(neg_taken, g + 1)
                sp.dma_start(q_op[MROW:MROW + 2, b, :, :].rearrange("r h (u q) -> r (h u) q", u=UT).bitcast(F32),
                             neg_t[:].bitcast(F32)).then_inc(m_filled, 16)

            sp.wait_ge(hi_taken, 2 * UT)
            sp.wait_ge(lo_taken, 2 * UT)
            fill(0, 0)
            fill_max(0, 0)

            def turn(j):
                for b in range(2):
                    g = 2 * j + b
                    if isinstance(g, int) and g == 0:
                        sp.wait_ge(hi_taken, 2 * TILES)
                        sp.wait_ge(lo_taken, 2 * TILES)
                    if isinstance(g, int) and g + 1 == NG:
                        break
                    wait(sp, qk_done, HG * KC * g)
                    fill(g + 1, 1 - b)
                    fill_max(g + 1, 1 - b)

            span(sp, 1, 1, PAIRS, turn)

            sp.wait_ge(att_ready, NG)
            sp.wait_ge(pv_done, NG * KC)
            sp.wait_ge(pairs_summed, NG * KC // 2)

            def slots(j):
                for u in range(4):
                    s = 4 * j + u
                    if has(s):
                        wait(sp, x1_ready, s - 3)
                        wait(sp, y_done, s - 3)
                        sp.dma_start(xe_in[:, u, :], x_t[:, bass.ds(s, 1), :]).then_inc(xe_loaded[u], 16)
                        src = att[:, bass.ds(4 * j, 4), u * P:(u + 1) * P]
                        sp.dma_start(att_t[:, u, :].rearrange("p (q n) -> p q n", q=KE), src).then_inc(att_loaded[u], 16)
                    if has(s - 4):
                        sp.wait_ge(o_ready, s - 3)
                        sp.dma_start(out_t[:, bass.ds(s - 4, 1), :], o_t[:, u % 2, :]).then_inc(stored[u % 2], 16)

            span(sp, 1, 1, SLOT_CHUNKS, slots)
            for s in stored:
                sp.wait_ge(s, 16 * TILES // 2)

        @block.gpsimd
        def _(pool):
            nc.gpsimd.memset(ones[:], 1.0).then_inc(const_set, 1)
            nc.gpsimd.memset(eps[:], EPS).then_inc(const_set, 1)
            pool.wait_ge(const_set, 2)
            nc.gpsimd.memset(k_op[MROW:MROW + 2, :].bitcast(F32), 1.0).then_inc(const_set, 1)
            pool.wait_ge(e_loaded, 64)
            pool.wait_ge(const_set, 3)
            for k in range(KE):
                nc.gpsimd.tensor_tensor(wffn[:, k, :], wffn[:, k, :], scale_b[:], ALU.mult).then_inc(scaled, 1)

            def turn(j):
                for i in range(KC):
                    n = j * KC + i
                    wait(pool, exp_done, 2 * HG * (n + 1))
                    wait(pool, den_done, n - 1)
                    c = 2 * i % PRING
                    nc.gpsimd.tensor_tensor(pair_sum[:, i % 2, :], probs[:, c, :], probs[:, c + 1, :],
                                            ALU.add).then_inc(pairs_summed, 1)

            span(pool, 1, 1, PAIRS, turn)

            def slots(j):
                for u in range(4):
                    s = 4 * j + u
                    if has(s - 1):
                        t, r = s - 1, (u - 1) % 4
                        pool.wait_ge(y_normed, t + 1)
                        pool.wait_ge(xe_loaded[r], 16 * ((j if r < 3 else j - 1) + 1))
                        wait(pool, xl2_ready, t - 3)
                        wait(pool, o_ready, t - 3)
                        nc.gpsimd.tensor_tensor(x1[:, r, :], xe_in[:, r, :], yn[:, (u - 1) % 2, :],
                                                ALU.add).then_inc(x1_ready, 1)
                    if has(s - 4):
                        pool.wait_ge(zn_ready, s - 3)
                        wait(pool, stored[u % 2], 16 * (2 * j - 2 + u // 2))
                        nc.gpsimd.tensor_tensor(o_t[:, u % 2, :], x1[:, u, :], zn[:, u % 2, :],
                                                ALU.add).then_inc(o_ready, 1)

            span(pool, 1, 1, SLOT_CHUNKS, slots)

        @block.scalar
        def _(act):
            act.wait_ge(const_set, 3)

            def slots_a(j):
                for u in range(4):
                    t = 4 * j + u
                    if has(t + 1):
                        v = (u + 1) % 2
                        act.wait_ge(x_turned, t + 2)
                        wait(act, qkv_done, t)
                        nc.scalar.activation(xT[:, v, :], s_ps[:, v, :], ACT.Copy).then_inc(xT_ready, 1)
                    if has(t):
                        act.wait_ge(qkv_done, t + 1)
                        nc.scalar.activation(v_sb[:, bass.ds(t, 1), :], mx_ps[:, u % 2, E + D:QKV].unsqueeze(1),
                                             ACT.Copy).then_inc(v_taken, 1)
                    if has(t - 1):
                        act.wait_ge(q_turned, t)
                        nc.scalar.activation(q_hi[q_part(t - 1, (u - 1) % 4)].bitcast(F32R),
                                             o_ps[:].rearrange("p (q n) -> p q n", q=KE), ACT.Copy).then_inc(hi_taken, 1)
                        nc.scalar.activation(k_op[0:QROWS, bass.ds((t - 1) * P, P)],
                                             den_ps[0:QROWS, 0:P], ACT.Copy).then_inc(hi_taken, 1)
                    if has(t + 4):
                        act.wait_ge(stats_a, t + 5)
                        nc.scalar.activation(sd_a[:, u:u + 1], mv_a[:, u, 1:2], ACT.Sqrt,
                                             bias=eps[:, 0:1]).then_inc(std_a, 1)

            span(act, 1, 2, NQB + 1, slots_a, start=-1)
            act.wait_ge(lo_taken, 2 * TILES)
            act.wait_ge(q_turned, TILES)

            def take_max(g):
                act.wait_ge(neg_turned, g + 1)
                wait(act, m_filled, 16 * g)
                nc.scalar.activation(neg_t[:], mx_ps[0:2 * HG * UT, 0, 0:P], ACT.Copy).then_inc(neg_taken, 1)

            def take(g):
                act.wait_ge(pv_done, (g + 1) * KC)
                wait(act, att_ready, g)
                nc.scalar.activation(o_sb[:], o_ps[:], ACT.Copy).then_inc(o_taken, 1)
                act.wait_ge(den_done, (g + 1) * KC // 2)
                nc.scalar.activation(den_sb[:], den_ps[:], ACT.Copy).then_inc(den_taken, 1)

            take_max(0)

            def turn(j):
                for i in range(2 * KC):
                    b, c = divmod(i, KC)
                    if c == TAKE_STEP and not (isinstance(j, int) and j == 0 and b == 0):
                        take(2 * j + b - 1)
                    n = j * 2 * KC + i
                    for h in range(HG):
                        act.wait_ge(qk_done, HG * n + h + 1)
                        if h == 0:
                            wait(act, pv_done, n - PRING + 1)
                            wait(act, pairs_summed, j * KC + (i // 2 - PRING // 2 + 1))
                        nc.scalar.activation(probs[:, i % PRING, h * QB:(h + 1) * QB], s_ps[:, h % 2, :],
                                             ACT.Exp, scale=SCALE).then_inc(exp_done, 1)
                    if c == TURN_STEP and not (isinstance(j, int) and 2 * j + b + 1 == NG):
                        take_max(2 * j + b + 1)

            span(act, 1, 1, PAIRS, turn)
            take(NG - 1)

            def std(stat, done, k, t, r):
                act.wait_ge(stat, t + 1)
                nc.scalar.activation(sd_e[:, k, r:r + 1], mv_e[:, k, r, 1:2], ACT.Sqrt,
                                     bias=eps[:, 0:1]).then_inc(done, 1)

            def slots(j):
                for u in range(4):
                    s = 4 * j + u
                    if has(s - 1):
                        std(y_stat, y_std, 0, s - 1, (u - 1) % 2)
                    if has(s - 2):
                        std(x1_stat, x1_std, 1, s - 2, u % 2)
                    if has(s - 3):
                        act.wait_ge(x2_turned, s - 2)
                        wait(act, z_done, s - 4)
                        nc.scalar.activation(x2T[:, (u - 3) % 2, :], s_ps[:, (u - 3) % 2, :],
                                             ACT.Copy).then_inc(x2T_ready, 1)
                    if has(s - 4):
                        std(z_stat, z_std, 2, s - 4, u % 2)
                    if has(s - 1):
                        act.wait_ge(y_coef, s)
                        wait(act, x1_ready, s - 2)
                        nc.scalar.activation(yn[:, (u - 1) % 2, :], mx_ps[:, (u - 1) % 2, 0:E], ACT.Identity,
                                             bias=nm_e[:, (u - 1) % 2:(u - 1) % 2 + 1],
                                             scale=rs_e[:, 0, (u - 1) % 2:(u - 1) % 2 + 1]).then_inc(y_normed, 1)

            span(act, 1, 1, SLOT_CHUNKS, slots)

        @block.vector
        def _(dve):

            def slots_a(j):
                for u in range(4):
                    t = 4 * j + u
                    if has(t + 3):
                        v = (u + 3) % 4
                        dve.wait_ge(std_a, t + 4)
                        nc.vector.reciprocal(rs_a[:, v:v + 1], sd_a[:, v:v + 1]).then_inc(inverse_a, 1)
                        dve.wait_ge(inverse_a, t + 4)
                        wait(dve, x_turned, t)
                        nc.vector.tensor_scalar(xln[:, v, :], x_in[:, v, :], mv_a[:, v, 0:1], rs_a[:, v:v + 1],
                                                ALU.subtract, ALU.mult).then_inc(normed, 1)
                    if has(t):
                        n = H + 1
                        src = mx_ps[:, u % 2, 0:E + D]
                        halves = src.rearrange("p (h two d) -> p h two d", two=2, d=D // 2)
                        rb = rot_b.rearrange("p (h two d) -> p h two d", two=2, d=D // 2)
                        cs = cos_sb[:, bass.ds(t, 1), :].to_broadcast([P, n, D])
                        sn = sin_sb[:, bass.ds(t, 1), :]
                        if isinstance(t, int) and t == 0:
                            dve.wait_ge(t_loaded, 48)
                        dve.wait_ge(qkv_done, t + 1)
                        dve.wait_ge(v_taken, t + 1)
                        wait(dve, rotated, 2 * t)
                        nc.vector.tensor_tensor(rot_a.rearrange("p (h d) -> p h d", d=D),
                                                src.rearrange("p (h d) -> p h d", d=D), cs,
                                                ALU.mult).then_inc(products, 1)
                        for half in range(2):
                            nc.vector.tensor_tensor(
                                rb[:, :, half, :], halves[:, :, 1 - half, :],
                                sn[:, :, half * D // 2:(half + 1) * D // 2].to_broadcast([P, n, D // 2]),
                                ALU.mult).then_inc(products, 1)
                        dve.wait_ge(products, 3 * t + 3)
                        wait(dve, q_turned, t - 1)
                        nc.vector.tensor_tensor(q_rot[:, u % 2, :], rot_a[:, 0:E], rot_b[:, 0:E],
                                                ALU.add).then_inc(rotated, 1)
                        nc.vector.tensor_tensor(k3[:, u % 2, :].rearrange("p (n d) -> p n d", n=3),
                                                rot_a[:, E:E + D].unsqueeze(1).to_broadcast([P, 3, D]),
                                                rot_b[:, E:E + D].unsqueeze(1).to_broadcast([P, 3, D]),
                                                ALU.add).then_inc(rotated, 1)
                    if has(t + 4):
                        dve.wait_ge(x_loaded[u], 16 * (j + 2))
                        nc.vector.bn_stats(st_a[:, u, :], x_in[:, u, :])
                        nc.vector.drain()
                        nc.vector.bn_aggr(mv_a[:, u, :], st_a[:, u, :]).then_inc(stats_a, 1)
                    if has(t - 1):
                        dve.wait_ge(hi_taken, 2 * t)
                        at = q_part(t - 1, (u - 1) % 4)
                        nc.vector.tensor_tensor(q_lo[at].bitcast(F32R), o_ps[:].rearrange("p (q n) -> p q n", q=KE),
                                                q_hi[at], ALU.subtract).then_inc(lo_taken, 1)
                        kl = k_op[D:2 * D, bass.ds((t - 1) * P, P)]
                        nc.vector.tensor_tensor(kl, den_ps[D:2 * D, 0:P], kl.bitcast(F32),
                                                ALU.subtract).then_inc(lo_taken, 1)

            span(dve, 1, 2, NQB + 1, slots_a, start=-1)

            def reduce_units(g, first, count):
                for k in range(first, first + count):
                    n = g * MAXUNITS + k
                    dve.wait_ge(mx_done, n + 1)
                    nc.vector.tensor_reduce(max_part[:, k // 2, k % 2:k % 2 + 1], mx_ps[:, k % 2, :], AX.X,
                                            ALU.max).then_inc(mx_reduced, 1)

            def negate(g):
                n = HG * UT
                dve.wait_ge(mx_reduced, (g + 1) * MAXUNITS)
                wait(dve, neg_turned, g)
                nc.vector.tensor_reduce(neg_max[:], max_part[:], AX.X, ALU.max, negate=True).then_inc(neg_ready, 1)
                dve.wait_ge(neg_ready, g + 1)
                nc.vector.tensor_copy(neg_parts[:, 0:n].bitcast(F32R), neg_max[:]).then_inc(neg_split, 1)
                dve.wait_ge(neg_split, 2 * g + 1)
                nc.vector.tensor_tensor(neg_parts[:, n:2 * n].bitcast(F32R), neg_max[:], neg_parts[:, 0:n],
                                        ALU.subtract).then_inc(neg_split, 1)

            def invert(g):
                dve.wait_ge(den_taken, g + 1)
                wait(dve, att_ready, g)
                nc.vector.reciprocal(rden[:], den_sb[:]).then_inc(den_inv, 1)

            def finish(g):
                dve.wait_ge(den_inv, g + 1)
                dve.wait_ge(o_taken, g + 1)
                nc.vector.tensor_tensor(att[:, bass.ds(g, 1), :], o_sb[:].unsqueeze(1), rden[:].unsqueeze(1),
                                        ALU.mult).then_inc(att_ready, 1)

            reduce_units(0, 0, MAXUNITS)
            negate(0)

            def turn(j):
                for b in range(2):
                    g = 2 * j + b
                    more = not (isinstance(g, int) and g + 1 == NG)
                    before = not (isinstance(g, int) and g == 0)
                    first = 0
                    for c in range(KC):
                        if more:
                            reduce_units(g + 1, first, MAX_PLAN[c])
                            first += MAX_PLAN[c]
                            if MAX_PLAN[c] and first == MAXUNITS:
                                negate(g + 1)
                        if c == TAKE_STEP and before:
                            invert(g - 1)
                        if c == TAKE_STEP + 1 and before:
                            finish(g - 1)

            span(dve, 1, 1, PAIRS, turn)
            invert(NG - 1)
            finish(NG - 1)

            def stats(src, k, r, stat, t):
                nc.vector.bn_stats(st_e[:, k, :], src)
                nc.vector.drain()
                nc.vector.bn_aggr(mv_e[:, k, r, :], st_e[:, k, :]).then_inc(stat, 1)

            def coef(k, r, done, coefs, t):
                dve.wait_ge(done, t + 1)
                nc.vector.reciprocal(rs_e[:, k, r:r + 1], sd_e[:, k, r:r + 1]).then_inc(coefs, 1)

            def slots(j):
                for u in range(4):
                    s = 4 * j + u
                    if has(s - 1):
                        t, r = s - 1, (u - 1) % 2
                        dve.wait_ge(y_done, t + 1)
                        wait(dve, y_normed, t - 1)
                        stats(mx_ps[:, r, 0:E], 0, r, y_stat, t)
                    if has(s - 2):
                        t, r = s - 2, u % 2
                        dve.wait_ge(x1_ready, t + 1)
                        wait(dve, xl2_ready, t - 1)
                        stats(x1[:, (u - 2) % 4, :], 1, r, x1_stat, t)
                    if has(s - 4):
                        t, r = s - 4, u % 2
                        dve.wait_ge(z_done, t + 1)
                        wait(dve, zn_ready, t)
                        nc.vector.tensor_tensor(zb[:, r, :], mx_ps[:, r, E:2 * E], bias_b[:], ALU.add).then_inc(z_biased, 1)
                        dve.wait_ge(z_biased, t + 1)
                        stats(zb[:, r, :], 2, r, z_stat, t)
                    if has(s - 1):
                        t, r = s - 1, (u - 1) % 2
                        dve.wait_ge(y_std, t + 1)
                        nc.vector.reciprocal(rs_e[:, 0, r:r + 1], sd_e[:, 0, r:r + 1]).then_inc(y_inv, 1)
                        dve.wait_ge(y_inv, t + 1)
                        nc.vector.tensor_scalar(nm_e[:, r:r + 1], mv_e[:, 0, r, 0:1], rs_e[:, 0, r:r + 1], -1.0,
                                                ALU.mult, ALU.mult).then_inc(y_coef, 1)
                    if has(s - 2):
                        t, r = s - 2, u % 2
                        coef(1, r, x1_std, x1_coef, t)
                        dve.wait_ge(x1_coef, t + 1)
                        wait(dve, x2_turned, t - 1)
                        nc.vector.tensor_scalar(xl2[:, r, :], x1[:, (u - 2) % 4, :], mv_e[:, 1, r, 0:1],
                                                rs_e[:, 1, r:r + 1], ALU.subtract, ALU.mult).then_inc(xl2_ready, 1)
                    if has(s - 4):
                        t, r = s - 4, u % 2
                        coef(2, r, z_std, z_coef, t)
                        dve.wait_ge(z_coef, t + 1)
                        wait(dve, o_ready, t)
                        nc.vector.tensor_scalar(zn[:, r, :], zb[:, r, :], mv_e[:, 2, r, 0:1],
                                                rs_e[:, 2, r:r + 1], ALU.subtract, ALU.mult).then_inc(zn_ready, 1)

            span(dve, 1, 1, SLOT_CHUNKS, slots)

        @block.tensor
        def _(pe):
            def turn_tile(dst, src):
                for k in range(KE):
                    last = nc.tensor.transpose(dst[:, k * P:(k + 1) * P], src[:, k * P:(k + 1) * P], ident[:])
                return last

            pe.wait_ge(t_loaded, 48)
            pe.wait_ge(w_loaded, 16)

            def slots_a(j):
                for u in range(4):
                    t = 4 * j + u
                    if has(t + 1):
                        v = (u + 1) % 4
                        pe.wait_ge(normed, t + 2)
                        wait(pe, xT_ready, t)
                        turn_tile(s_ps[:, v % 2, :], xln[:, v, :]).then_inc(x_turned, 1)
                    if has(t):
                        pe.wait_ge(xT_ready, t + 1)
                        wait(pe, rotated, 2 * t - 2)
                        wait(pe, v_taken, t - 1)
                        for cols in (slice(0, E), slice(E, QKV)):
                            for k in range(KE):
                                last = nc.tensor.matmul(mx_ps[:, u % 2, cols], xT[:, u % 2, k * P:(k + 1) * P],
                                                        wqkv[:, k, cols], start=(k == 0), stop=(k == KE - 1))
                        last.then_inc(qkv_done, 1)
                    if has(t - 1):
                        v = (u - 1) % 2
                        pe.wait_ge(rotated, 2 * t)
                        wait(pe, lo_taken, 2 * t - 2)
                        turn_tile(o_ps[:], q_rot[:, v, :])
                        nc.tensor.transpose(den_ps[0:QROWS, 0:P], k3[:, v, :], ident[:]).then_inc(q_turned, 1)

            span(pe, 1, 2, NQB + 1, slots_a, start=-1)

            def max_unit(g, b, k, fills):
                h, u, keys = k // (2 * UT), k // 2 % UT, k % 2 * 2 * QB
                if k % (2 * UT) == 0:
                    pe.wait_ge(q_filled[b][h], 16 * FILLS * fills)
                wait(pe, mx_reduced, g * MAXUNITS + k - 1)
                for half in range(2):
                    mm = nc.tensor.matmul(mx_ps[:, k % 2, half * QB:(half + 1) * QB],
                                          q_op[0:QROWS, b, h, u * P:(u + 1) * P],
                                          k_op[0:QROWS, keys + half * QB:keys + (half + 1) * QB],
                                          start=True, stop=True)
                mm.then_inc(mx_done, 1)

            def turn_max(g):
                pe.wait_ge(neg_split, 2 * (g + 1))
                nc.tensor.transpose(mx_ps[0:2 * HG * UT, 0, 0:P], neg_parts[:], ident[:]).then_inc(neg_turned, 1)

            def scores(n, b, c, h):
                wait(pe, exp_done, HG * n + h - 1)
                nc.tensor.matmul(s_ps[:, h % 2, :], k_op[:, c * P:(c + 1) * P], q_op[:, b, h, :],
                                 start=True, stop=True).then_inc(qk_done, 1)

            def weighted_sum(n, c):
                pe.wait_ge(exp_done, HG * (n + 1))
                for h in range(HG):
                    last = nc.tensor.matmul(o_ps[h * D:(h + 1) * D, :], v_sb[:, c, :],
                                            probs[:, c % PRING, h * QB:(h + 1) * QB],
                                            start=(c == 0), stop=(c == KC - 1))
                last.then_inc(pv_done, 1)

            def total(n, i):
                pe.wait_ge(pairs_summed, n + 1)
                for h in range(HG):
                    last = nc.tensor.matmul(den_ps[h * D:(h + 1) * D, :], ones[:],
                                            pair_sum[:, i % 2, h * QB:(h + 1) * QB],
                                            start=(i == 0), stop=(i == KC // 2 - 1))
                last.then_inc(den_done, 1)

            def lagged(g, c):
                if c == 0:
                    wait(pe, o_taken, g)
                weighted_sum(g * KC + c, c)

            def lagged_total(g, c):
                if c % 2:
                    if c == 1:
                        wait(pe, den_taken, g)
                    total(g * (KC // 2) + c // 2, c // 2)

            pe.wait_ge(const_set, 3)
            pe.wait_ge(lo_taken, 2 * TILES)
            pe.wait_ge(hi_taken, 2 * TILES)
            for k in range(MAXUNITS):
                max_unit(0, 0, k, 1)
            turn_max(0)

            def turn(j):
                for b in range(2):
                    g = 2 * j + b
                    more = not (isinstance(g, int) and g + 1 == NG)
                    first = 0
                    pe.wait_ge(m_filled, 16 * (g + 1))
                    for c in range(KC):
                        units = [first + k for k in range(MAX_PLAN[c] if more else 0)]
                        if units and first == 0:
                            pe.wait_ge(neg_taken, g + 1)
                        first += len(units)
                        if c >= PV_LAG:
                            late = (g, c - PV_LAG)
                        else:
                            late = (g - 1, KC + c - PV_LAG) if not (isinstance(g, int) and g == 0) else None

                        def unit():
                            if units:
                                max_unit(g + 1, 1 - b, units.pop(0), j + 1 + b)

                        n = g * KC + c
                        scores(n, b, c, 0)
                        if len(units) > 3:
                            unit()
                        scores(n, b, c, 1)
                        if late:
                            lagged(*late)
                        if c == TURN_STEP and more:
                            turn_max(g + 1)
                        scores(n, b, c, 2)
                        unit()
                        scores(n, b, c, 3)
                        unit()
                        if late:
                            lagged_total(*late)
                        unit()
                        assert not units

            span(pe, 1, 1, PAIRS, turn)
            for c in range(KC - PV_LAG, KC):
                lagged(NG - 1, c)
                lagged_total(NG - 1, c)

            pe.wait_ge(scaled, KE)
            pe.wait_ge(e_loaded, 64)

            def slots(j):
                for u in range(4):
                    s = 4 * j + u
                    if has(s - 3):
                        t = s - 3
                        pe.wait_ge(xl2_ready, t + 1)
                        wait(pe, x2T_ready, t - 1)
                        turn_tile(s_ps[:, (u - 3) % 2, :], xl2[:, (u - 3) % 2, :]).then_inc(x2_turned, 1)
                    if has(s):
                        pe.wait_ge(att_loaded[u], 16 * (j + 1))
                        wait(pe, y_normed, s - 1)
                        for k in range(KE):
                            last = nc.tensor.matmul(mx_ps[:, u % 2, 0:E], att_t[:, u, k * P:(k + 1) * P],
                                                    wout[:, k, :], start=(k == 0), stop=(k == KE - 1))
                        last.then_inc(y_done, 1)
                    if has(s - 3):
                        t, r = s - 3, (u - 3) % 2
                        pe.wait_ge(x2T_ready, t + 1)
                        wait(pe, z_biased, t - 1)
                        for k in range(KE):
                            last = nc.tensor.matmul(mx_ps[:, r, E:2 * E], x2T[:, r, k * P:(k + 1) * P],
                                                    wffn[:, k, :], start=(k == 0), stop=(k == KE - 1))
                        last.then_inc(z_done, 1)

            span(pe, 1, 1, SLOT_CHUNKS, slots)


def kernel(**inputs):
    import numpy as np
    import concourse.bacc as bacc
    from concourse.bass_utils import run_bass_kernel_spmd

    pos = (10000.0 ** ((-2.0 * np.arange(0, D, 2) - 1.0) / D)).astype(np.float32)
    angles = np.arange(T, dtype=np.float32)[:, None] * pos[None, :]
    cos = np.concatenate([np.cos(angles), np.cos(angles)], axis=1)
    sin = np.concatenate([-np.sin(angles), np.sin(angles)], axis=1)

    def by_tile(a):
        return np.ascontiguousarray(a.reshape(TILES, P, D).transpose(1, 0, 2))

    arrays = {
        "x": np.ascontiguousarray(inputs["L0_attn_x"]),
        "w_qkv_t": np.ascontiguousarray(np.asarray(inputs["L0_attn_w_attn"]).T),
        "w_out_t": np.ascontiguousarray(np.asarray(inputs["L0_attn_w_out"]).T),
        "w_ffn_t": np.ascontiguousarray(np.asarray(inputs["L0_ffn_weight"]).T),
        "ffn_scale": np.ascontiguousarray(inputs["L0_ffn_scale_weight"]),
        "ffn_bias": np.ascontiguousarray(inputs["L0_ffn_bias"]),
        "cos": by_tile(cos),
        "sin": by_tile(sin),
        "eye": np.eye(P, dtype=np.float32),
    }
    nc = bacc.Bacc("TRN2", target_bir_lowering=False, num_devices=1)
    args = [nc.dram_tensor(n, a.shape, mybir.dt.from_np(a.dtype), kind="ExternalInput").ap() for n, a in arrays.items()]
    out = nc.dram_tensor("out", (1, T, E), F32, kind="ExternalOutput").ap()
    build(nc, *args, out)
    r = run_bass_kernel_spmd(nc, [arrays], core_ids=[0])
    return r.results[0]["out"]
```

```python
from contextlib import ExitStack

import concourse.bass as bass
from concourse import mybir

F32 = mybir.dt.float32
F32R = mybir.dt.float32r
ALU = mybir.AluOpType
ACT = mybir.ActivationFunctionType
AX = mybir.AxisListType

P = 128
T = 2048
E = 512
D = 32
H = E // D
QKV = E + 2 * D
HH = QKV // D // 2
KE = E // P
TILES = T // P
QB = 512
NQB = T // QB
UT = QB // P
HG = P // D
NG = NQB * H // HG
KC = T // P
KB = T // QB
QROWS = 3 * D
MROW = QROWS
AROWS = QROWS + 2
SCALE = float(D) ** -0.5
EPS = 1e-5

PV_LAG = 4
PRING = 8
MAXUNITS = HG * UT * KB // 2
SUM_ENDS = [2, 5, 8, 11, 13, 15]
SUMS = len(SUM_ENDS)
SUM_STARTS = [0] + [end + 1 for end in SUM_ENDS[:-1]]
TRIPLES = sum(end - start == 2 for start, end in zip(SUM_STARTS, SUM_ENDS))
assert SUM_ENDS[-1] == KC - 1 and SUMS % 2 == 0
STEPS = ("wsstss", "uusswsusu", "swsusus", "wssuustsu",
         "suswss", "uusstssw", "sswss", "uusswss",
         "uusswsus", "uswsusus", "wsususs", "ustsususw",
         "sususwus", "sususwsu", "sustssw", "sstssw")
UNITS = [step.count("u") for step in STEPS]
LATE_TOTALS = sum(step.count("t") for step in STEPS[:PV_LAG])
assert len(STEPS) == KC and sum(UNITS) == MAXUNITS and all(s.count("s") == HG and s.count("w") == 1 for s in STEPS)
assert sum(step.count("t") for step in STEPS) == SUMS
TAKE_STEP = PV_LAG
SPLIT_STEP = 7
TURN_STEP = 14
EARLY_UNITS = 2
FILLS = 3


def build(nc, x, w_qkv_t, w_out_t, w_ffn_t, ffn_scale, ffn_bias, cos, sin, eye, out):
    x_t = x.rearrange("b (t p) e -> p (b t) e", p=P)
    out_t = out.rearrange("b (t p) e -> p (b t) e", p=P)

    with ExitStack() as ctx:
        def sb(name, shape, dt=F32):
            return ctx.enter_context(nc.sbuf_tensor(name, shape, dt))

        def psum(name, shape):
            return ctx.enter_context(nc.psum_tensor(name, shape, F32))

        def sem(name):
            return ctx.enter_context(nc.semaphore(name))

        bias_b = sb("bias_b", [P, E])
        wout_hi = sb("wout_hi", [P, KE, E], F32R)
        wout_lo = sb("wout_lo", [P, KE, E], F32R)
        wffn = sb("wffn", [P, KE, E])
        ident = sb("ident", [P, P])
        ones = sb("ones", [P, D])
        eps = sb("eps", [P, 1])
        q_hi = sb("q_hi", [P, NG, QB])
        q_lo = sb("q_lo", [P, NG, QB])
        att_hi, att_lo = q_hi, q_lo
        k_op = sb("k_op", [AROWS, T], F32R)
        v_sb = sb("v_sb", [P, KC, D])
        neg_parts = sb("neg_parts", [P, 2 * HG * UT])
        neg_t = sb("neg_t", [2 * HG * UT, P], F32R)
        max_part = sb("max_part", [P, HG * UT, KB // 2])
        neg_max = sb("neg_max", [P, HG * UT])
        o_sb = sb("o_sb", [P, QB])
        den_sb = sb("den_sb", [P, QB])
        rden = sb("rden", [P, QB])
        st = sb("st", [P, 4, 4, 6])
        mv = sb("mv", [P, 4, 4, 2])
        sd = sb("sd", [P, 4, 4])
        rs = sb("rs", [P, 4, 4])
        nm = sb("nm", [P, 4, 4])

        with ExitStack() as scope:
            def sc(name, shape, dt=F32):
                return scope.enter_context(nc.sbuf_tensor(name, shape, dt))

            wffn_hi = sc("wffn_hi", [P, KE, E], F32R)
            x2T_hi = sc("x2T_hi", [P, 2, E], F32R)
            x2T_lo = sc("x2T_lo", [P, 2, E], F32R)
            att_t = sc("att_t", [P, 4, 2, E], F32R)
            xe_in = sc("xe_in", [P, 4, E])
            wffn_lo = sc("wffn_lo", [P, KE, E], F32R)
            x1 = sc("x1", [P, 4, E])
            yn = sc("yn", [P, 2, E])
            xl2 = sc("xl2", [P, 2, E])
            zb = sc("zb", [P, 2, E])
            zn = sc("zn", [P, 2, E])
            o_t = sc("o_t", [P, 4, E])
        q_op = sb("q_op", [AROWS, 2, HG, QB], F32R)
        with ExitStack() as scope:
            def sa(name, shape, dt=F32):
                return scope.enter_context(nc.sbuf_tensor(name, shape, dt))

            x_in = sa("x_in", [P, 4, E])
            xln = sa("xln", [P, 4, E])
            xT_hi = sa("xT_hi", [P, 2, E], F32R)
            xT_lo = sa("xT_lo", [P, 2, E], F32R)
            q_rot = sa("q_rot", [P, 2, E])
            k3 = sa("k3", [P, 2, QROWS])
            rot_a = sa("rot_a", [P, 2, QKV])
            rot_b = sa("rot_b", [P, 2, QKV])
            wqkv = sa("wqkv", [P, KE, QKV])
            wqkv_hi = sa("wqkv_hi", [P, KE, QKV], F32R)
            wqkv_lo = sa("wqkv_lo", [P, KE, QKV], F32R)
            wout = sa("wout", [P, KE, E])
            scale_b = sa("scale_b", [P, E])
            cos_sb = sa("cos_sb", [P, TILES, D])
            sin_sb = sa("sin_sb", [P, TILES, D])
        probs = sb("probs", [P, PRING, HG * QB])
        chunk_sum = sb("chunk_sum", [P, 2, HG * QB])

        s_ps = psum("s_ps", [P, 2, QB])
        mx_ps = psum("mx_ps", [P, 2, 2 * QB])
        o_ps = psum("o_ps", [P, QB])
        den_ps = psum("den_ps", [P, QB])

        w_loaded = [sem(f"w_loaded{k}") for k in range(KE)]
        ident_loaded = sem("ident_loaded")
        angles_loaded = sem("angles_loaded")
        e_loaded = sem("e_loaded")
        wout_loaded = sem("wout_loaded")
        x_loaded = [sem(f"x_loaded{u}") for u in range(4)]
        const_set = sem("const_set")
        scaled = sem("scaled")
        w_hi_ready = sem("w_hi_ready")
        w_lo_ready = sem("w_lo_ready")
        wout_split = sem("wout_split")
        inverse_a = sem("inverse_a")
        coef_a = sem("coef_a")
        products = sem("products")
        stats_a = sem("stats_a")
        std_a = sem("std_a")
        normed = sem("normed")
        x_turned = sem("x_turned")
        xT_hi_ready = sem("xT_hi_ready")
        xT_ready = sem("xT_ready")
        qkv_done = sem("qkv_done")
        v_taken = sem("v_taken")
        rotated = sem("rotated")
        q_turned = sem("q_turned")
        hi_taken = sem("hi_taken")
        lo_taken = sem("lo_taken")

        q_filled = [[sem(f"q_filled{b}_{h}") for h in range(HG)] for b in range(2)]
        mx_done = sem("mx_done")
        mx_reduced = sem("mx_reduced")
        neg_ready = sem("neg_ready")
        neg_split = sem("neg_split")
        neg_turned = sem("neg_turned")
        neg_taken = sem("neg_taken")
        m_filled = sem("m_filled")
        qk_done = sem("qk_done")
        exp_done = sem("exp_done")
        pv_done = sem("pv_done")
        two_summed = sem("two_summed")
        chunks_summed = sem("chunks_summed")
        last_two_summed = sem("last_two_summed")
        last_summed = sem("last_summed")
        den_done = sem("den_done")
        o_taken = sem("o_taken")
        den_taken = sem("den_taken")
        den_inv = sem("den_inv")
        att_whole = sem("att_whole")
        att_ready = sem("att_ready")

        xe_loaded = [sem(f"xe_loaded{i}") for i in range(4)]
        att_loaded = [sem(f"att_loaded{i}") for i in range(4)]
        y_done = sem("y_done")
        stat_e = [sem(f"stat_e{n}") for n in range(3)]
        std_e = [sem(f"std_e{n}") for n in range(3)]
        inverse_e = [sem(f"inverse_e{n}") for n in range(3)]
        coef_e = [sem(f"coef_e{n}") for n in range(3)]
        y_normed = sem("y_normed")
        x1_ready = sem("x1_ready")
        xl2_ready = sem("xl2_ready")
        x2_turned = sem("x2_turned")
        x2T_hi_ready = sem("x2T_hi_ready")
        x2T_ready = sem("x2T_ready")
        z_done = sem("z_done")
        z_biased = sem("z_biased")
        zn_ready = sem("zn_ready")
        o_ready = sem("o_ready")
        wffn_split = sem("wffn_split")
        stored = [sem(f"stored{i}") for i in range(4)]

        def wait(eng, s, n):
            if not isinstance(n, int) or n > 0:
                eng.wait_ge(s, n)

        def span(eng, first, last, end, body, start=0):
            first = max(first, start)
            for i in range(start, first):
                body(i)
            if end - last > first:
                with eng.Fori(first, end - last) as i:
                    body(i)
            for i in range(max(first, end - last), end):
                body(i)

        PAIRS = NG // 2
        SLOT_CHUNKS = NQB + 1
        TAIL = PRING // 2
        LAST_SLOT = 0

        def q_part(t, u):
            return (slice(None), bass.ds(t - u, HG), slice(u * P, (u + 1) * P))

        def sum_of(c):
            return next(i for i, end in enumerate(SUM_ENDS) if c <= end)

        def unit_at(g, k):
            if isinstance(g, int) and g == 0:
                return k % (MAXUNITS // 2) // UT, k % UT, k // (MAXUNITS // 2)
            return k // (2 * UT), k // 2 % UT, k % 2

        def unit_room(g, k):
            if isinstance(g, int) and g == 0 and k % 3 == 2:
                return s_ps[:].rearrange("p b n -> p (b n)")
            return mx_ps[:, k % 3 if isinstance(g, int) and g == 0 else k % 2, :]

        def score_room(r):
            return s_ps[:].rearrange("p b n -> p (b n)") if r % 3 == 2 else mx_ps[:, r % 3, :]

        def wait_sums(eng, g, i):
            if isinstance(g, int) and g == NG - 1:
                wait(eng, chunks_summed, g * SUMS + i // 2 + 1)
                wait(eng, last_summed, (i + 1) // 2)
            else:
                wait(eng, chunks_summed, g * SUMS + i + 1)

        def add_chunks(eng, on, g, b, i, two, whole, triples):
            start, end = SUM_STARTS[i], SUM_ENDS[i]
            at = chunk_sum[:, i % 2, :]
            ring = [(b * KC + c) % PRING for c in range(start, end + 1)]
            eng.wait_ge(exp_done, HG * (g * KC + start + 2))
            wait(eng, den_done, g * SUMS + i - 1)
            first = on.tensor_tensor(at, probs[:, ring[0], :], probs[:, ring[1], :], ALU.add)
            if len(ring) == 3:
                first.then_inc(two, 1)
                eng.wait_ge(two, triples + 1)
                eng.wait_ge(exp_done, HG * (g * KC + end + 1))
                on.tensor_tensor(at, at, probs[:, ring[2], :], ALU.add).then_inc(whole, 1)
            else:
                first.then_inc(whole, 1)

        def qkv_ps(slot):
            return mx_ps[:, slot, :].rearrange("p (b n) -> p b n", b=2)[:, :, 0:HH * D]

        def has(tile):
            return not isinstance(tile, int) or 0 <= tile < TILES

        block = ctx.enter_context(nc.Block())

        @block.sync
        def _(sp):
            def load_x(t, u):
                sp.dma_start(x_in[:, u, :], x_t[:, bass.ds(t, 1), :]).then_inc(x_loaded[u], 16)

            load_x(0, 0)
            sp.dma_start(ident[:], eye).then_inc(ident_loaded, 16)
            load_x(1, 1)
            for k in range(KE):
                sp.dma_start(wqkv[:, k, :], w_qkv_t[k * P:(k + 1) * P, :]).then_inc(w_loaded[k], 16)
            load_x(2, 2)
            load_x(3, 3)
            sp.dma_start(cos_sb[:], cos).then_inc(angles_loaded, 16)
            sp.dma_start(sin_sb[:], sin).then_inc(angles_loaded, 16)

            def reload(j):
                for u in range(4):
                    sp.wait_ge(normed, 4 * j + u - 3)
                    load_x(4 * j + u, u)

            span(sp, 2, 0, NQB, reload, start=1)
            sp.dma_start(wout[:], w_out_t.rearrange("(k p) n -> p k n", p=P)).then_inc(wout_loaded, 16)
            sp.dma_start(wffn[:], w_ffn_t.rearrange("(k p) n -> p k n", p=P)).then_inc(e_loaded, 16)
            sp.dma_start(scale_b[:], ffn_scale.partition_broadcast(P)).then_inc(e_loaded, 16)
            sp.dma_start(bias_b[:], ffn_bias.partition_broadcast(P)).then_inc(e_loaded, 16)

            def fill(g, b):
                for h in range(HG):
                    rows = slice(h * D, (h + 1) * D)
                    for at, part in enumerate((q_hi, q_hi, q_lo)):
                        sp.dma_start(q_op[at * D:(at + 1) * D, b, h, :].bitcast(F32),
                                     part[rows, bass.ds(g, 1), :]).then_inc(q_filled[b][h], 16)

            def fill_max(g, b):
                sp.wait_ge(neg_taken, g + 1)
                sp.dma_start(q_op[MROW:MROW + 2, b, :, :].rearrange("r h (u q) -> r (h u) q", u=UT).bitcast(F32),
                             neg_t[:].bitcast(F32)).then_inc(m_filled, 16)

            sp.wait_ge(hi_taken, 2 * UT)
            sp.wait_ge(lo_taken, 2 * UT)
            fill(0, 0)
            fill_max(0, 0)

            def turn(j):
                for b in range(2):
                    g = 2 * j + b
                    if isinstance(g, int) and g == 0:
                        sp.wait_ge(hi_taken, 2 * TILES)
                        sp.wait_ge(lo_taken, 2 * TILES)
                    if isinstance(g, int) and g + 1 == NG:
                        break
                    wait(sp, qk_done, HG * KC * g)
                    fill(g + 1, 1 - b)
                    fill_max(g + 1, 1 - b)

            span(sp, 1, 1, PAIRS, turn)

            sp.wait_ge(pv_done, NG * KC - TAIL)
            wait_sums(sp, NG - 1, sum_of(KC - TAIL - 1))

            def slots(j):
                for u in range(4):
                    s = 4 * j + u
                    if has(s):
                        if u == 0:
                            sp.wait_ge(att_ready, 2 * HG * (j + 1))
                        wait(sp, y_done, s - 3)
                        for at, part in enumerate((att_hi, att_lo)):
                            sp.dma_start(att_t[:, u, at, :].rearrange("p (q n) -> p q n", q=KE).bitcast(F32),
                                         part[:, bass.ds(4 * j, 4), u * P:(u + 1) * P]).then_inc(att_loaded[u], 16)
                        wait(sp, x1_ready, s - 3)
                        sp.dma_start(xe_in[:, u, :], x_t[:, bass.ds(s, 1), :]).then_inc(xe_loaded[u], 16)
                    if has(s - 8):
                        sp.wait_ge(o_ready, s - 7)
                        sp.dma_start(out_t[:, bass.ds(s - 8, 1), :], o_t[:, u, :]).then_inc(stored[u], 16)

            span(sp, 2, 2, SLOT_CHUNKS + 1, slots)
            for s in stored:
                sp.wait_ge(s, 16 * TILES // 4)

        @block.gpsimd
        def _(pool):
            nc.gpsimd.memset(ones[:], 1.0).then_inc(const_set, 1)
            nc.gpsimd.memset(eps[:], EPS).then_inc(const_set, 1)
            pool.wait_ge(const_set, 2)
            nc.gpsimd.memset(k_op[MROW:MROW + 2, :].bitcast(F32), 1.0).then_inc(const_set, 1)

            def slots_a(j):
                for u in range(4):
                    t = 4 * j + u
                    v = u % 2
                    pool.wait_ge(products, 3 * t + 3)
                    wait(pool, q_turned, t - 1)
                    nc.gpsimd.tensor_tensor(q_rot[:, v, :], rot_a[:, v, 0:E], rot_b[:, v, 0:E],
                                            ALU.add).then_inc(rotated, 1)
                    nc.gpsimd.tensor_tensor(k3[:, v, :].rearrange("p (n d) -> p n d", n=3),
                                            rot_a[:, v, E:E + D].unsqueeze(1).to_broadcast([P, 3, D]),
                                            rot_b[:, v, E:E + D].unsqueeze(1).to_broadcast([P, 3, D]),
                                            ALU.add).then_inc(rotated, 1)

            span(pool, 1, 0, NQB, slots_a)
            pool.wait_ge(e_loaded, 48)
            for k in range(KE):
                nc.gpsimd.tensor_tensor(wffn[:, k, :], wffn[:, k, :], scale_b[:], ALU.mult).then_inc(scaled, 1)

            def turn(j):
                for b in range(2):
                    g = 2 * j + b
                    mine = range(0, SUMS, 2 if isinstance(g, int) and g == NG - 1 else 1)
                    triples = 0
                    for i in mine:
                        add_chunks(pool, nc.gpsimd, g, b, i, two_summed, chunks_summed, g * TRIPLES + triples)
                        triples += SUM_ENDS[i] - SUM_STARTS[i] == 2

            pool.wait_ge(wout_split, 1)
            nc.gpsimd.tensor_tensor(wout_lo[:], wout[:], wout_hi[:].bitcast(F32), ALU.subtract).then_inc(wout_split, 1)
            pool.wait_ge(wout_split, 2)
            pool.wait_ge(q_turned, TILES)
            span(pool, 1, 1, PAIRS, turn)

            def slots(j):
                for u in range(4):
                    s = 4 * j + u
                    if has(s - 1):
                        t, r = s - 1, (u - 1) % 4
                        pool.wait_ge(y_normed, t + 1)
                        pool.wait_ge(xe_loaded[r], 16 * ((j if r < 3 else j - 1) + 1))
                        wait(pool, xl2_ready, t - 3)
                        wait(pool, o_ready, t - 3)
                        nc.gpsimd.tensor_tensor(x1[:, r, :], xe_in[:, r, :], yn[:, (u - 1) % 2, :],
                                                ALU.add).then_inc(x1_ready, 1)
                    if has(s - 4):
                        pool.wait_ge(zn_ready, s - 3)
                        wait(pool, stored[u], 16 * (j - 1))
                        nc.gpsimd.tensor_tensor(o_t[:, u, :], x1[:, u, :], zn[:, u % 2, :],
                                                ALU.add).then_inc(o_ready, 1)

            span(pool, 1, 1, SLOT_CHUNKS, slots)

        @block.scalar
        def _(act):
            act.wait_ge(const_set, 3)

            def split_hi(hi, whole, done):
                nc.scalar.activation(hi, whole, ACT.Copy).then_inc(done, 1)

            def standard(k, slot, stat, done, n):
                act.wait_ge(stat, n)
                nc.scalar.activation(sd[:, k, slot:slot + 1], mv[:, k, slot, 1:2], ACT.Sqrt,
                                     bias=eps[:, 0:1]).then_inc(done, 1)

            def normed_to(dst, src, k, slot, done):
                nc.scalar.activation(dst, src, ACT.Identity, bias=nm[:, k, slot:slot + 1],
                                     scale=rs[:, k, slot:slot + 1]).then_inc(done, 1)

            def slots_a(j):
                for u in range(4):
                    t = 4 * j + u
                    if has(t + 1):
                        v = (u + 1) % 2
                        act.wait_ge(x_turned, t + 2)
                        wait(act, qkv_done, t)
                        nc.scalar.activation(xT_hi[:, v, :], s_ps[:, v, :], ACT.Copy).then_inc(xT_hi_ready, 1)
                    if has(t - 2):
                        act.wait_ge(q_turned, t - 1)
                        nc.scalar.activation(q_hi[q_part(t - 2, (u - 2) % 4)].bitcast(F32R),
                                             o_ps[:].rearrange("p (q n) -> p q n", q=KE),
                                             ACT.Copy).then_inc(hi_taken, 1)
                        nc.scalar.activation(k_op[0:QROWS, bass.ds((t - 2) * P, P)],
                                             den_ps[0:QROWS, 0:P], ACT.Copy).then_inc(hi_taken, 1)
                    if has(t + 3):
                        standard(0, (u + 3) % 4, stats_a, std_a, t + 4)
                    if has(t + 2):
                        v = (u + 2) % 4
                        act.wait_ge(coef_a, t + 3)
                        wait(act, x_turned, t - 1)
                        normed_to(xln[:, v, :], x_in[:, v, :], 0, v, normed)
                    if isinstance(t, int) and t == -1:
                        for k in range(KE):
                            act.wait_ge(w_loaded[k], 16)
                            split_hi(wqkv_hi[:, k, :], wqkv[:, k, :], w_hi_ready)
                    if has(t):
                        act.wait_ge(qkv_done, t + 1)
                        nc.scalar.activation(v_sb[:, bass.ds(t, 1), :], qkv_ps(u % 2)[:, 1:2, (HH - 1) * D:HH * D],
                                             ACT.Copy).then_inc(v_taken, 1)

            span(act, 1, 2, NQB + 1, slots_a, start=-1)
            act.wait_ge(wout_loaded, 16)
            split_hi(wout_hi[:], wout[:], wout_split)
            act.wait_ge(lo_taken, 2 * TILES)
            act.wait_ge(q_turned, TILES)
            act.wait_ge(wout_split, 2)
            act.wait_ge(scaled, KE)

            def take_max(g):
                act.wait_ge(neg_turned, g + 1)
                wait(act, m_filled, 16 * g)
                nc.scalar.activation(neg_t[:], mx_ps[0:2 * HG * UT, 0, 0:P], ACT.Copy).then_inc(neg_taken, 1)

            def take(g):
                act.wait_ge(pv_done, (g + 1) * KC)
                wait(act, att_ready, 2 * g)
                nc.scalar.activation(o_sb[:], o_ps[:], ACT.Copy).then_inc(o_taken, 1)
                act.wait_ge(den_done, (g + 1) * SUMS)
                nc.scalar.activation(den_sb[:], den_ps[:], ACT.Copy).then_inc(den_taken, 1)

            take_max(0)

            def round_att(g):
                act.wait_ge(att_whole, g + 1)
                nc.scalar.activation(att_hi[:, bass.ds(g, 1), :].bitcast(F32R), o_sb[:].unsqueeze(1),
                                     ACT.Copy).then_inc(att_ready, 1)

            def turn(j):
                for i in range(2 * KC):
                    b, c = divmod(i, KC)
                    if isinstance(j, int) and j == PAIRS - 1 and b == 1 and c == 1:
                        split_hi(wffn_hi[:], wffn[:], wffn_split)
                    if c == SPLIT_STEP and not (isinstance(j, int) and j == 0 and b == 0):
                        round_att(2 * j + b - 1)
                    if c == TAKE_STEP and not (isinstance(j, int) and j == 0 and b == 0):
                        take(2 * j + b - 1)
                    n = j * 2 * KC + i
                    wait(act, pv_done, n - PRING + 1)
                    wait_sums(act, 2 * j + b - (c < PRING), sum_of((c - PRING) % KC))
                    if isinstance(j, int) and 2 * j + b == NG - 1:
                        for h in range(0, HG, 2):
                            act.wait_ge(qk_done, HG * n + h + 2)
                            nc.scalar.activation(probs[:, i % PRING, h * QB:(h + 2) * QB],
                                                 score_room(c * HG // 2 + h // 2),
                                                 ACT.Exp, scale=SCALE).then_inc(exp_done, 2)
                    else:
                        for h in range(HG):
                            act.wait_ge(qk_done, HG * n + h + 1)
                            nc.scalar.activation(probs[:, i % PRING, h * QB:(h + 1) * QB], s_ps[:, h % 2, :],
                                                 ACT.Exp, scale=SCALE).then_inc(exp_done, 1)
                    if c == TURN_STEP and not (isinstance(j, int) and 2 * j + b + 1 == NG):
                        take_max(2 * j + b + 1)

            span(act, 1, 1, PAIRS, turn)
            take(NG - 1)

            def slots(j):
                for u in range(4):
                    s = 4 * j + u
                    if isinstance(s, int) and s == LAST_SLOT + 1:
                        round_att(NG - 1)
                    if has(s - 1):
                        standard(1, (u - 1) % 4, stat_e[0], std_e[0], s)
                    if has(s - 2):
                        standard(2, (u - 2) % 4, stat_e[1], std_e[1], s - 1)
                    if has(s - 3):
                        r = (u - 3) % 2
                        act.wait_ge(x2_turned, s - 2)
                        wait(act, z_done, s - 4)
                        nc.scalar.activation(x2T_hi[:, r, :], s_ps[:, r, :], ACT.Copy).then_inc(x2T_hi_ready, 1)
                    if has(s - 1):
                        r = (u - 1) % 2
                        act.wait_ge(coef_e[0], s)
                        wait(act, x1_ready, s - 2)
                        normed_to(yn[:, r, :], mx_ps[:, r, 0:E], 1, (u - 1) % 4, y_normed)
                    if has(s - 2):
                        act.wait_ge(coef_e[1], s - 1)
                        wait(act, x2_turned, s - 3)
                        normed_to(xl2[:, u % 2, :], x1[:, (u - 2) % 4, :], 2, (u - 2) % 4, xl2_ready)
                    if has(s - 4):
                        standard(3, u, stat_e[2], std_e[2], s - 3)
                        act.wait_ge(coef_e[2], s - 3)
                        wait(act, o_ready, s - 4)
                        normed_to(zn[:, u % 2, :], zb[:, u % 2, :], 3, u, zn_ready)

            span(act, 1, 1, SLOT_CHUNKS, slots)

        @block.vector
        def _(dve):

            def split_lo(lo, whole, hi, done):
                nc.vector.tensor_tensor(lo, whole, hi.bitcast(F32), ALU.subtract).then_inc(done, 1)

            def statistics(k, slot, src, stat):
                nc.vector.bn_stats(st[:, k, slot, :], src)
                nc.vector.drain()
                nc.vector.bn_aggr(mv[:, k, slot, :], st[:, k, slot, :]).then_inc(stat, 1)

            def coefficients(k, slot, std, inverse, coef, n):
                dve.wait_ge(std, n)
                nc.vector.reciprocal(rs[:, k, slot:slot + 1], sd[:, k, slot:slot + 1]).then_inc(inverse, 1)
                dve.wait_ge(inverse, n)
                nc.vector.tensor_scalar(nm[:, k, slot:slot + 1], mv[:, k, slot, 0:1], rs[:, k, slot:slot + 1], -1.0,
                                        ALU.mult, ALU.mult).then_inc(coef, 1)

            def reduce_units(g, first, count):
                for k in range(first, first + count):
                    n = g * MAXUNITS + k
                    dve.wait_ge(mx_done, n + 1)
                    h, u, keys = unit_at(g, k)
                    nc.vector.tensor_reduce(max_part[:, h * UT + u, keys:keys + 1], unit_room(g, k), AX.X,
                                            ALU.max).then_inc(mx_reduced, 1)

            def slots_a(j):
                for u in range(4):
                    t = 4 * j + u
                    if has(t + 2):
                        coefficients(0, (u + 2) % 4, std_a, inverse_a, coef_a, t + 3)
                    if has(t + 1):
                        v = (u + 1) % 2
                        dve.wait_ge(xT_hi_ready, t + 2)
                        split_lo(xT_lo[:, v, :], s_ps[:, v, :], xT_hi[:, v, :], xT_ready)
                    if isinstance(t, int) and t == -1:
                        for k in range(KE):
                            dve.wait_ge(w_hi_ready, k + 1)
                            split_lo(wqkv_lo[:, k, :], wqkv[:, k, :], wqkv_hi[:, k, :], w_lo_ready)
                    if has(t - 2):
                        dve.wait_ge(hi_taken, 2 * t - 2)
                        at = q_part(t - 2, (u - 2) % 4)
                        q_whole = o_ps[:].rearrange("p (q n) -> p q n", q=KE)
                        split_lo(q_lo[at].bitcast(F32R), q_whole, q_hi[at], lo_taken)
                        kl = k_op[D:2 * D, bass.ds((t - 2) * P, P)]
                        split_lo(kl, den_ps[D:2 * D, 0:P], kl, lo_taken)
                    if has(t + 4):
                        dve.wait_ge(x_loaded[u], 16 * (j + 2))
                        wait(dve, coef_a, t + 1)
                        wait(dve, normed, t + 1)
                        statistics(0, u, x_in[:, u, :], stats_a)
                    if has(t):
                        v = u % 2
                        src = qkv_ps(v).rearrange("p b (h d) -> p b h d", d=D)
                        ra, rb = (r[:, v, :].rearrange("p (b h d) -> p b h d", b=2, d=D) for r in (rot_a, rot_b))
                        cs, sn = (r[:, bass.ds(t, 1), :].unsqueeze(1) for r in (cos_sb, sin_sb))
                        if isinstance(t, int) and t == 0:
                            dve.wait_ge(angles_loaded, 32)
                        dve.wait_ge(qkv_done, t + 1)
                        dve.wait_ge(v_taken, t + 1)
                        wait(dve, rotated, 2 * t - 2)
                        nc.vector.tensor_tensor(ra, src, cs.to_broadcast([P, 2, HH, D]), ALU.mult).then_inc(products, 1)
                        for half in range(2):
                            to, other = (slice(i * D // 2, (i + 1) * D // 2) for i in (half, 1 - half))
                            nc.vector.tensor_tensor(rb[:, :, :, to], src[:, :, :, other],
                                                    sn[:, :, :, to].to_broadcast([P, 2, HH, D // 2]),
                                                    ALU.mult).then_inc(products, 1)
                    if isinstance(t, int) and t == TILES:
                        reduce_units(0, 0, EARLY_UNITS)

            span(dve, 1, 2, NQB + 1, slots_a, start=-1)

            def negate(g):
                n = HG * UT
                dve.wait_ge(mx_reduced, (g + 1) * MAXUNITS)
                wait(dve, neg_turned, g)
                nc.vector.tensor_reduce(neg_max[:], max_part[:], AX.X, ALU.max, negate=True).then_inc(neg_ready, 1)
                dve.wait_ge(neg_ready, g + 1)
                nc.vector.tensor_copy(neg_parts[:, 0:n].bitcast(F32R), neg_max[:]).then_inc(neg_split, 1)
                dve.wait_ge(neg_split, 2 * g + 1)
                nc.vector.tensor_tensor(neg_parts[:, n:2 * n].bitcast(F32R), neg_max[:], neg_parts[:, 0:n],
                                        ALU.subtract).then_inc(neg_split, 1)

            def invert(g):
                dve.wait_ge(den_taken, g + 1)
                wait(dve, att_whole, g)
                nc.vector.reciprocal(rden[:], den_sb[:]).then_inc(den_inv, 1)

            def finish(g):
                dve.wait_ge(den_inv, g + 1)
                dve.wait_ge(o_taken, g + 1)
                nc.vector.tensor_tensor(o_sb[:], o_sb[:], rden[:], ALU.mult).then_inc(att_whole, 1)

            def finish_lo(g):
                dve.wait_ge(att_ready, 2 * g + 1)
                at = (slice(None), bass.ds(g, 1), slice(None))
                split_lo(att_lo[at].bitcast(F32R), o_sb[:].unsqueeze(1), att_hi[at], att_ready)

            reduce_units(0, EARLY_UNITS, MAXUNITS - EARLY_UNITS)
            negate(0)

            def turn(j):
                for b in range(2):
                    g = 2 * j + b
                    more = not (isinstance(g, int) and g + 1 == NG)
                    before = not (isinstance(g, int) and g == 0)
                    first = 0
                    for c in range(KC):
                        if more:
                            reduce_units(g + 1, first, UNITS[c])
                            first += UNITS[c]
                            if UNITS[c] and first == MAXUNITS:
                                negate(g + 1)
                        if not more and c in SUM_ENDS[1::2]:
                            i = sum_of(c)
                            add_chunks(dve, nc.vector, g, b, i, last_two_summed, last_summed, i // 2)
                        if c == TAKE_STEP and before:
                            invert(g - 1)
                            finish(g - 1)
                        if c == SPLIT_STEP and before:
                            finish_lo(g - 1)

            span(dve, 1, 1, PAIRS, turn)
            dve.wait_ge(wffn_split, 1)
            dve.wait_ge(pv_done, NG * KC - TAIL)
            wait_sums(dve, NG - 1, sum_of(KC - TAIL - 1))
            split_lo(wffn_lo[:], wffn[:], wffn_hi[:], wffn_split)

            def slots(j):
                for u in range(4):
                    s = 4 * j + u
                    if isinstance(s, int) and s == LAST_SLOT:
                        invert(NG - 1)
                        finish(NG - 1)
                    if isinstance(s, int) and s == LAST_SLOT + 1:
                        finish_lo(NG - 1)
                    if has(s - 1):
                        dve.wait_ge(y_done, s)
                        statistics(1, (u - 1) % 4, mx_ps[:, (u - 1) % 2, 0:E], stat_e[0])
                    if has(s - 2):
                        dve.wait_ge(x1_ready, s - 1)
                        statistics(2, (u - 2) % 4, x1[:, (u - 2) % 4, :], stat_e[1])
                    if has(s - 1):
                        coefficients(1, (u - 1) % 4, std_e[0], inverse_e[0], coef_e[0], s)
                    if has(s - 2):
                        coefficients(2, (u - 2) % 4, std_e[1], inverse_e[1], coef_e[1], s - 1)
                    if has(s - 3):
                        r = (u - 3) % 2
                        dve.wait_ge(x2T_hi_ready, s - 2)
                        split_lo(x2T_lo[:, r, :], s_ps[:, r, :], x2T_hi[:, r, :], x2T_ready)
                    if has(s - 4):
                        dve.wait_ge(z_done, s - 3)
                        wait(dve, zn_ready, s - 4)
                        nc.vector.tensor_tensor(zb[:, u % 2, :], mx_ps[:, u % 2, E:2 * E], bias_b[:],
                                                ALU.add).then_inc(z_biased, 1)
                        dve.wait_ge(z_biased, s - 3)
                        statistics(3, u, zb[:, u % 2, :], stat_e[2])
                        coefficients(3, u, std_e[2], inverse_e[2], coef_e[2], s - 3)

            span(dve, 1, 1, SLOT_CHUNKS, slots)

        @block.tensor
        def _(pe):
            def turn_tile(dst, src):
                for k in range(KE):
                    last = nc.tensor.transpose(dst[:, k * P:(k + 1) * P], src[:, k * P:(k + 1) * P], ident[:])
                return last

            def product(dst, lhs, rhs, ready=None):
                for k in range(KE):
                    if ready is not None:
                        pe.wait_ge(ready, k + 1)
                    for n, (a, b) in enumerate(((0, 0), (0, 1), (1, 0))):
                        last = nc.tensor.matmul(dst, lhs(a, k), rhs(b, k), start=(k == 0 and n == 0),
                                                stop=(k == KE - 1 and n == 2))
                return last

            def block_k(parts, *at):
                return lambda part, k: parts[part][(slice(None), *at, slice(k * P, (k + 1) * P))]

            def max_unit(g, b, k, fills):
                h, u, keys = unit_at(g, k)
                if u == 0 and keys == 0:
                    pe.wait_ge(q_filled[b][h], 16 * FILLS * fills)
                rooms = 3 if isinstance(g, int) and g == 0 else 2
                wait(pe, mx_reduced, g * MAXUNITS + k - rooms + 1)
                if isinstance(g, int) and g == 0 and k == 2:
                    pe.wait_ge(xT_ready, TILES)
                for half in range(2):
                    mm = nc.tensor.matmul(unit_room(g, k)[:, half * QB:(half + 1) * QB],
                                          q_op[0:QROWS, b, h, u * P:(u + 1) * P],
                                          k_op[0:QROWS, bass.ds((2 * keys + half) * QB, QB)],
                                          start=True, stop=True)
                mm.then_inc(mx_done, 1)

            pe.wait_ge(ident_loaded, 16)

            def slots_a(j):
                for u in range(4):
                    t = 4 * j + u
                    if has(t + 1):
                        v = (u + 1) % 4
                        pe.wait_ge(normed, t + 2)
                        wait(pe, xT_ready, t)
                        turn_tile(s_ps[:, v % 2, :], xln[:, v, :]).then_inc(x_turned, 1)
                    if has(t - 2):
                        v = u % 2
                        pe.wait_ge(rotated, 2 * t - 2)
                        wait(pe, lo_taken, 2 * t - 4)
                        turn_tile(o_ps[:], q_rot[:, v, :])
                        nc.tensor.transpose(den_ps[0:QROWS, 0:P], k3[:, v, :], ident[:]).then_inc(q_turned, 1)
                    if has(t):
                        pe.wait_ge(xT_ready, t + 1)
                        wait(pe, rotated, 2 * t - 2)
                        wait(pe, v_taken, t - 1)
                        for half in range(2):
                            cols = slice(half * HH * D, (half + 1) * HH * D)
                            last = product(qkv_ps(u % 2)[:, half, :], block_k((xT_hi, xT_lo), u % 2),
                                           lambda part, k: (wqkv_hi, wqkv_lo)[part][:, k, cols],
                                           w_lo_ready if isinstance(t, int) and t == 0 else None)
                        last.then_inc(qkv_done, 1)
                    if isinstance(t, int) and t == TILES:
                        pe.wait_ge(const_set, 3)
                        pe.wait_ge(lo_taken, TILES)
                        pe.wait_ge(hi_taken, TILES)
                        for k in range(EARLY_UNITS):
                            pe.wait_ge(products, 3 * (TILES - 1 + k))
                            max_unit(0, 0, k, 1)

            span(pe, 1, 2, NQB + 1, slots_a, start=-1)

            def turn_max(g):
                pe.wait_ge(neg_split, 2 * (g + 1))
                nc.tensor.transpose(mx_ps[0:2 * HG * UT, 0, 0:P], neg_parts[:], ident[:]).then_inc(neg_turned, 1)

            def scores(n, b, c, h):
                if isinstance(n, int) and n >= (NG - 1) * KC:
                    r = c * HG // 2 + h // 2
                    pe.wait_ge(exp_done, HG * KC * (NG - 1) + 2 * max(r - 2, 0))
                    dst = score_room(r)[:, h % 2 * QB:(h % 2 + 1) * QB]
                else:
                    wait(pe, exp_done, HG * n + h - 1)
                    dst = s_ps[:, h % 2, :]
                nc.tensor.matmul(dst, k_op[:, c * P:(c + 1) * P], q_op[:, b, h, :],
                                 start=True, stop=True).then_inc(qk_done, 1)

            def weighted_sum(g, c):
                if c == 0:
                    wait(pe, o_taken, g)
                pe.wait_ge(exp_done, HG * (g * KC + c + 1))
                for h in range(HG):
                    last = nc.tensor.matmul(o_ps[h * D:(h + 1) * D, :], v_sb[:, c, :],
                                            probs[:, c % PRING, h * QB:(h + 1) * QB],
                                            start=(c == 0), stop=(c == KC - 1))
                last.then_inc(pv_done, 1)

            def total(g, i):
                if i == 0:
                    wait(pe, den_taken, g)
                wait_sums(pe, g, i)
                for h in range(HG):
                    last = nc.tensor.matmul(den_ps[h * D:(h + 1) * D, :], ones[:],
                                            chunk_sum[:, i % 2, h * QB:(h + 1) * QB],
                                            start=(i == 0), stop=(i == SUMS - 1))
                last.then_inc(den_done, 1)

            for k in range(EARLY_UNITS, MAXUNITS):
                if k == MAXUNITS // 2:
                    pe.wait_ge(lo_taken, 2 * TILES)
                    pe.wait_ge(hi_taken, 2 * TILES)
                max_unit(0, 0, k, 1)
            turn_max(0)

            def turn(j):
                for b in range(2):
                    g = 2 * j + b
                    more = not (isinstance(g, int) and g + 1 == NG)
                    before = not (isinstance(g, int) and g == 0)
                    totals = -LATE_TOTALS
                    unit = 0
                    pe.wait_ge(m_filled, 16 * (g + 1))
                    for c, step in enumerate(STEPS):
                        h = 0
                        for what in step:
                            if what == "s":
                                scores(g * KC + c, b, c, h)
                                h += 1
                            elif what == "w" and c >= PV_LAG:
                                weighted_sum(g, c - PV_LAG)
                            elif what == "w" and before:
                                weighted_sum(g - 1, KC + c - PV_LAG)
                            elif what == "t":
                                if totals >= 0:
                                    total(g, totals)
                                elif before:
                                    total(g - 1, SUMS + totals)
                                totals += 1
                            elif what == "u" and more:
                                if unit == 0:
                                    pe.wait_ge(neg_taken, g + 1)
                                max_unit(g + 1, 1 - b, unit, j + 1 + b)
                                unit += 1
                        if c == TURN_STEP and more:
                            turn_max(g + 1)

            span(pe, 1, 1, PAIRS, turn)
            for c in range(KC - PV_LAG, KC):
                weighted_sum(NG - 1, c)
            for i in range(SUMS - LATE_TOTALS, SUMS):
                total(NG - 1, i)

            pe.wait_ge(wout_split, 2)

            def slots(j):
                for u in range(4):
                    s = 4 * j + u
                    if has(s - 3):
                        t = s - 3
                        pe.wait_ge(xl2_ready, t + 1)
                        wait(pe, x2T_ready, t - 1)
                        turn_tile(s_ps[:, (u - 3) % 2, :], xl2[:, (u - 3) % 2, :]).then_inc(x2_turned, 1)
                    if has(s):
                        pe.wait_ge(att_loaded[u], 32 * (j + 1))
                        wait(pe, y_normed, s - 1)
                        last = product(mx_ps[:, u % 2, 0:E],
                                       lambda part, k: att_t[:, u, part, k * P:(k + 1) * P],
                                       lambda part, k: (wout_hi, wout_lo)[part][:, k, :])
                        last.then_inc(y_done, 1)
                    if has(s - 3):
                        t, r = s - 3, (u - 3) % 2
                        pe.wait_ge(x2T_ready, t + 1)
                        wait(pe, z_biased, t - 1)
                        if isinstance(t, int) and t == 0:
                            pe.wait_ge(wffn_split, 2)
                        last = product(mx_ps[:, r, E:2 * E], block_k((x2T_hi, x2T_lo), r),
                                       lambda part, k: (wffn_hi, wffn_lo)[part][:, k, :])
                        last.then_inc(z_done, 1)

            span(pe, 1, 1, SLOT_CHUNKS, slots)


def kernel(**inputs):
    import numpy as np
    import concourse.bacc as bacc
    from concourse.bass_utils import run_bass_kernel_spmd

    pos = (10000.0 ** ((-2.0 * np.arange(0, D, 2) - 1.0) / D)).astype(np.float32)
    angles = np.arange(T, dtype=np.float32)[:, None] * pos[None, :]
    cos = np.concatenate([np.cos(angles), np.cos(angles)], axis=1)
    sin = np.concatenate([-np.sin(angles), np.sin(angles)], axis=1)

    def by_tile(a):
        return np.ascontiguousarray(a.reshape(TILES, P, D).transpose(1, 0, 2))

    arrays = {
        "x": np.ascontiguousarray(inputs["L0_attn_x"]),
        "w_qkv_t": np.ascontiguousarray(np.asarray(inputs["L0_attn_w_attn"]).T),
        "w_out_t": np.ascontiguousarray(np.asarray(inputs["L0_attn_w_out"]).T),
        "w_ffn_t": np.ascontiguousarray(np.asarray(inputs["L0_ffn_weight"]).T),
        "ffn_scale": np.ascontiguousarray(inputs["L0_ffn_scale_weight"]),
        "ffn_bias": np.ascontiguousarray(inputs["L0_ffn_bias"]),
        "cos": by_tile(cos),
        "sin": by_tile(sin),
        "eye": np.eye(P, dtype=np.float32),
    }
    nc = bacc.Bacc("TRN2", target_bir_lowering=False, num_devices=1)
    args = [nc.dram_tensor(n, a.shape, mybir.dt.from_np(a.dtype), kind="ExternalInput").ap() for n, a in arrays.items()]
    out = nc.dram_tensor("out", (1, T, E), F32, kind="ExternalOutput").ap()
    build(nc, *args, out)
    r = run_bass_kernel_spmd(nc, [arrays], core_ids=[0])
    return r.results[0]["out"]
```
